# Optimizing a Trainium2 kernel written in Bass

```python
import numpy as np
import jax
import jax.numpy as jnp

def _softmax(x, axis=-1):
    return jax.nn.softmax(x, axis=axis)

def _gelu(x):
    return jax.nn.gelu(x, approximate=True)

def _silu(x):
    return jax.nn.silu(x)

def _sigmoid(x):
    return jax.nn.sigmoid(x)

def _layernorm(x, axis=-1, eps=1e-05):
    m = jnp.mean(x, axis=axis, keepdims=True)
    v = jnp.var(x, axis=axis, keepdims=True)
    return (x - m) / jnp.sqrt(v + eps)

def _scatter_add(tgt, idx, src, axis=0):
    return tgt.at[idx].add(src)

def _segment_sum(src, seg, n):
    return jax.ops.segment_sum(src, seg, n)
kernel_name = 'mk_dlrm_tower_d1_rec_r8_d5648b'

def setup_inputs(seed: int=0):
    np.random.seed(seed)
    _w = jnp.asarray

    def _rec_inputs():
        import jax
        import jax.numpy as jnp
        _tk = jax.random.key(seed)
        dense_ctx = jax.random.normal(jax.random.fold_in(_tk, 190), (512, 16), jnp.float32)
        ids = jnp.stack([jax.random.randint(jax.random.fold_in(_tk, 200 + f), (512,), 0, v, jnp.int32) for f, v in enumerate([12500, 12500, 1250, 12500, 125000, 12500, 12500, 1000, 1250, 1000, 1250, 1250, 125000, 12500, 12500, 1000, 1250, 1000, 1000, 1000, 12500, 1000, 1000, 1250, 12500, 1000, 1000, 1250, 1250, 1000, 125000, 125000, 12500, 1000, 12500, 1000, 125000, 125000, 1000, 1000])], axis=1)
        tbl_0 = 0.05 * jax.random.normal(jax.random.fold_in(_tk, 500 + 0), (12500, 32), jnp.float32)
        tbl_1 = 0.05 * jax.random.normal(jax.random.fold_in(_tk, 500 + 1), (12500, 32), jnp.float32)
        tbl_2 = 0.05 * jax.random.normal(jax.random.fold_in(_tk, 500 + 2), (1250, 32), jnp.float32)
        tbl_3 = 0.05 * jax.random.normal(jax.random.fold_in(_tk, 500 + 3), (12500, 32), jnp.float32)
        tbl_4 = 0.05 * jax.random.normal(jax.random.fold_in(_tk, 500 + 4), (125000, 32), jnp.float32)
        tbl_5 = 0.05 * jax.random.normal(jax.random.fold_in(_tk, 500 + 5), (12500, 32), jnp.float32)
        tbl_6 = 0.05 * jax.random.normal(jax.random.fold_in(_tk, 500 + 6), (12500, 32), jnp.float32)
        tbl_7 = 0.05 * jax.random.normal(jax.random.fold_in(_tk, 500 + 7), (1000, 32), jnp.float32)
        tbl_8 = 0.05 * jax.random.normal(jax.random.fold_in(_tk, 500 + 8), (1250, 32), jnp.float32)
        tbl_9 = 0.05 * jax.random.normal(jax.random.fold_in(_tk, 500 + 9), (1000, 32), jnp.float32)
        tbl_10 = 0.05 * jax.random.normal(jax.random.fold_in(_tk, 500 + 10), (1250, 32), jnp.float32)
        tbl_11 = 0.05 * jax.random.normal(jax.random.fold_in(_tk, 500 + 11), (1250, 32), jnp.float32)
        tbl_12 = 0.05 * jax.random.normal(jax.random.fold_in(_tk, 500 + 12), (125000, 32), jnp.float32)
        tbl_13 = 0.05 * jax.random.normal(jax.random.fold_in(_tk, 500 + 13), (12500, 32), jnp.float32)
        tbl_14 = 0.05 * jax.random.normal(jax.random.fold_in(_tk, 500 + 14), (12500, 32), jnp.float32)
        tbl_15 = 0.05 * jax.random.normal(jax.random.fold_in(_tk, 500 + 15), (1000, 32), jnp.float32)
        tbl_16 = 0.05 * jax.random.normal(jax.random.fold_in(_tk, 500 + 16), (1250, 32), jnp.float32)
        tbl_17 = 0.05 * jax.random.normal(jax.random.fold_in(_tk, 500 + 17), (1000, 32), jnp.float32)
        tbl_18 = 0.05 * jax.random.normal(jax.random.fold_in(_tk, 500 + 18), (1000, 32), jnp.float32)
        tbl_19 = 0.05 * jax.random.normal(jax.random.fold_in(_tk, 500 + 19), (1000, 32), jnp.float32)
        tbl_20 = 0.05 * jax.random.normal(jax.random.fold_in(_tk, 500 + 20), (12500, 32), jnp.float32)
        tbl_21 = 0.05 * jax.random.normal(jax.random.fold_in(_tk, 500 + 21), (1000, 32), jnp.float32)
        tbl_22 = 0.05 * jax.random.normal(jax.random.fold_in(_tk, 500 + 22), (1000, 32), jnp.float32)
        tbl_23 = 0.05 * jax.random.normal(jax.random.fold_in(_tk, 500 + 23), (1250, 32), jnp.float32)
        tbl_24 = 0.05 * jax.random.normal(jax.random.fold_in(_tk, 500 + 24), (12500, 32), jnp.float32)
        tbl_25 = 0.05 * jax.random.normal(jax.random.fold_in(_tk, 500 + 25), (1000, 32), jnp.float32)
        tbl_26 = 0.05 * jax.random.normal(jax.random.fold_in(_tk, 500 + 26), (1000, 32), jnp.float32)
        tbl_27 = 0.05 * jax.random.normal(jax.random.fold_in(_tk, 500 + 27), (1250, 32), jnp.float32)
        tbl_28 = 0.05 * jax.random.normal(jax.random.fold_in(_tk, 500 + 28), (1250, 32), jnp.float32)
        tbl_29 = 0.05 * jax.random.normal(jax.random.fold_in(_tk, 500 + 29), (1000, 32), jnp.float32)
        tbl_30 = 0.05 * jax.random.normal(jax.random.fold_in(_tk, 500 + 30), (125000, 32), jnp.float32)
        tbl_31 = 0.05 * jax.random.normal(jax.random.fold_in(_tk, 500 + 31), (125000, 32), jnp.float32)
        tbl_32 = 0.05 * jax.random.normal(jax.random.fold_in(_tk, 500 + 32), (12500, 32), jnp.float32)
        tbl_33 = 0.05 * jax.random.normal(jax.random.fold_in(_tk, 500 + 33), (1000, 32), jnp.float32)
        tbl_34 = 0.05 * jax.random.normal(jax.random.fold_in(_tk, 500 + 34), (12500, 32), jnp.float32)
        tbl_35 = 0.05 * jax.random.normal(jax.random.fold_in(_tk, 500 + 35), (1000, 32), jnp.float32)
        tbl_36 = 0.05 * jax.random.normal(jax.random.fold_in(_tk, 500 + 36), (125000, 32), jnp.float32)
        tbl_37 = 0.05 * jax.random.normal(jax.random.fold_in(_tk, 500 + 37), (125000, 32), jnp.float32)
        tbl_38 = 0.05 * jax.random.normal(jax.random.fold_in(_tk, 500 + 38), (1000, 32), jnp.float32)
        tbl_39 = 0.05 * jax.random.normal(jax.random.fold_in(_tk, 500 + 39), (1000, 32), jnp.float32)
        _rk = jax.random.fold_in(_tk, 7)
        W_top1 = 0.049029 * jax.random.normal(jax.random.fold_in(_tk, 801), (416, 512), jnp.float32)
        W_top2 = 0.0441942 * jax.random.normal(jax.random.fold_in(_tk, 802), (512, 256), jnp.float32)
        W_top3 = 0.0625 * jax.random.normal(jax.random.fold_in(_tk, 803), (256, 1), jnp.float32)
        b_top1 = jnp.zeros((512,), jnp.float32)
        b_top2 = jnp.zeros((256,), jnp.float32)
        return (dense_ctx, ids, tbl_0, tbl_1, tbl_2, tbl_3, tbl_4, tbl_5, tbl_6, tbl_7, tbl_8, tbl_9, tbl_10, tbl_11, tbl_12, tbl_13, tbl_14, tbl_15, tbl_16, tbl_17, tbl_18, tbl_19, tbl_20, tbl_21, tbl_22, tbl_23, tbl_24, tbl_25, tbl_26, tbl_27, tbl_28, tbl_29, tbl_30, tbl_31, tbl_32, tbl_33, tbl_34, tbl_35, tbl_36, tbl_37, tbl_38, tbl_39, W_top1, b_top1, W_top2, b_top2, W_top3)
    dense_ctx, ids, tbl_0, tbl_1, tbl_2, tbl_3, tbl_4, tbl_5, tbl_6, tbl_7, tbl_8, tbl_9, tbl_10, tbl_11, tbl_12, tbl_13, tbl_14, tbl_15, tbl_16, tbl_17, tbl_18, tbl_19, tbl_20, tbl_21, tbl_22, tbl_23, tbl_24, tbl_25, tbl_26, tbl_27, tbl_28, tbl_29, tbl_30, tbl_31, tbl_32, tbl_33, tbl_34, tbl_35, tbl_36, tbl_37, tbl_38, tbl_39, W_top1, b_top1, W_top2, b_top2, W_top3 = _rec_inputs()

    def _L0_rec_setup():
        import jax, jax.numpy as jnp
        import numpy as np
        B, F0, K = (256, 40, 32)
        CIN_SIZE = [200, 200]

        def _cin(inputs, params):
            Bb, F0_, Kk = inputs.shape
            res = inputs
            outs = []
            for wq, wk, wv, cw in params:
                x0_wk = inputs * wk
                x0_wv = inputs * wv
                xi_wq = res * wq
                phi = jnp.einsum('bfk,bgk->bkfg', x0_wk, xi_wq)
                alpha = jax.nn.softmax(phi, axis=2)
                x = alpha * jnp.transpose(x0_wv, (0, 2, 1))[:, :, :, None]
                x = x.reshape(Bb, Kk, -1)
                out = jnp.einsum('bkc,cj->bjk', x, cw[0])
                outs.append(out)
                res = out
            cat = jnp.concatenate(outs, axis=1)
            return cat.sum(axis=-1)
        key = jax.random.key(seed)
        ks = jax.random.split(key, 1 + 4 * len(CIN_SIZE))
        field_num = [F0] + CIN_SIZE
        d = {'inputs': jax.random.normal(ks[0], (B, F0, K), dtype=jnp.float32)}
        for i in range(len(CIN_SIZE)):
            d[f'wq{i}'] = jax.random.normal(ks[1 + 4 * i], (1, field_num[i], K), dtype=jnp.float32) * 0.05
            d[f'wk{i}'] = jax.random.normal(ks[2 + 4 * i], (1, F0, K), dtype=jnp.float32) * 0.05
            d[f'wv{i}'] = jax.random.normal(ks[3 + 4 * i], (1, F0, K), dtype=jnp.float32) * 0.05
            lim = (6.0 / (F0 * field_num[i] + field_num[i + 1])) ** 0.5
            d[f'cw{i}'] = jax.random.uniform(ks[4 + 4 * i], (1, F0 * field_num[i], field_num[i + 1]), minval=-lim, maxval=lim, dtype=jnp.float32)
        return d
    _L0_rec_all = _L0_rec_setup()
    _L0_rec_in = {k: v for k, v in _L0_rec_all.items() if k in ('wq0', 'wk0', 'wv0', 'cw0', 'wq1', 'wk1', 'wv1', 'cw1')}
    del _L0_rec_all
    return {'dense_ctx': dense_ctx, 'ids': ids, 'tbl_0': tbl_0, 'tbl_1': tbl_1, 'tbl_2': tbl_2, 'tbl_3': tbl_3, 'tbl_4': tbl_4, 'tbl_5': tbl_5, 'tbl_6': tbl_6, 'tbl_7': tbl_7, 'tbl_8': tbl_8, 'tbl_9': tbl_9, 'tbl_10': tbl_10, 'tbl_11': tbl_11, 'tbl_12': tbl_12, 'tbl_13': tbl_13, 'tbl_14': tbl_14, 'tbl_15': tbl_15, 'tbl_16': tbl_16, 'tbl_17': tbl_17, 'tbl_18': tbl_18, 'tbl_19': tbl_19, 'tbl_20': tbl_20, 'tbl_21': tbl_21, 'tbl_22': tbl_22, 'tbl_23': tbl_23, 'tbl_24': tbl_24, 'tbl_25': tbl_25, 'tbl_26': tbl_26, 'tbl_27': tbl_27, 'tbl_28': tbl_28, 'tbl_29': tbl_29, 'tbl_30': tbl_30, 'tbl_31': tbl_31, 'tbl_32': tbl_32, 'tbl_33': tbl_33, 'tbl_34': tbl_34, 'tbl_35': tbl_35, 'tbl_36': tbl_36, 'tbl_37': tbl_37, 'tbl_38': tbl_38, 'tbl_39': tbl_39, 'W_top1': W_top1, 'b_top1': b_top1, 'W_top2': W_top2, 'b_top2': b_top2, 'W_top3': W_top3, 'L0_rec_wq0': _L0_rec_in['wq0'], 'L0_rec_wk0': _L0_rec_in['wk0'], 'L0_rec_wv0': _L0_rec_in['wv0'], 'L0_rec_cw0': _L0_rec_in['cw0'], 'L0_rec_wq1': _L0_rec_in['wq1'], 'L0_rec_wk1': _L0_rec_in['wk1'], 'L0_rec_wv1': _L0_rec_in['wv1'], 'L0_rec_cw1': _L0_rec_in['cw1']}

def reference(dense_ctx, ids, tbl_0, tbl_1, tbl_2, tbl_3, tbl_4, tbl_5, tbl_6, tbl_7, tbl_8, tbl_9, tbl_10, tbl_11, tbl_12, tbl_13, tbl_14, tbl_15, tbl_16, tbl_17, tbl_18, tbl_19, tbl_20, tbl_21, tbl_22, tbl_23, tbl_24, tbl_25, tbl_26, tbl_27, tbl_28, tbl_29, tbl_30, tbl_31, tbl_32, tbl_33, tbl_34, tbl_35, tbl_36, tbl_37, tbl_38, tbl_39, W_top1, b_top1, W_top2, b_top2, W_top3, L0_rec_wq0, L0_rec_wk0, L0_rec_wv0, L0_rec_cw0, L0_rec_wq1, L0_rec_wk1, L0_rec_wv1, L0_rec_cw1):
    import jax
    import jax.numpy as jnp

    def _L0_rec_ref(inputs, wq0, wk0, wv0, cw0, wq1, wk1, wv1, cw1):
        import jax, jax.numpy as jnp
        import numpy as np
        B, F0, K = (256, 40, 32)
        CIN_SIZE = [200, 200]

        def _cin(inputs, params):
            Bb, F0_, Kk = inputs.shape
            res = inputs
            outs = []
            for wq, wk, wv, cw in params:
                x0_wk = inputs * wk
                x0_wv = inputs * wv
                xi_wq = res * wq
                phi = jnp.einsum('bfk,bgk->bkfg', x0_wk, xi_wq)
                alpha = jax.nn.softmax(phi, axis=2)
                x = alpha * jnp.transpose(x0_wv, (0, 2, 1))[:, :, :, None]
                x = x.reshape(Bb, Kk, -1)
                out = jnp.einsum('bkc,cj->bjk', x, cw[0])
                outs.append(out)
                res = out
            cat = jnp.concatenate(outs, axis=1)
            return cat.sum(axis=-1)
        return _cin(inputs, [(wq0, wk0, wv0, cw0), (wq1, wk1, wv1, cw1)])
    e = jnp.stack([tbl_0[ids[:, 0]], tbl_1[ids[:, 1]], tbl_2[ids[:, 2]], tbl_3[ids[:, 3]], tbl_4[ids[:, 4]], tbl_5[ids[:, 5]], tbl_6[ids[:, 6]], tbl_7[ids[:, 7]], tbl_8[ids[:, 8]], tbl_9[ids[:, 9]], tbl_10[ids[:, 10]], tbl_11[ids[:, 11]], tbl_12[ids[:, 12]], tbl_13[ids[:, 13]], tbl_14[ids[:, 14]], tbl_15[ids[:, 15]], tbl_16[ids[:, 16]], tbl_17[ids[:, 17]], tbl_18[ids[:, 18]], tbl_19[ids[:, 19]], tbl_20[ids[:, 20]], tbl_21[ids[:, 21]], tbl_22[ids[:, 22]], tbl_23[ids[:, 23]], tbl_24[ids[:, 24]], tbl_25[ids[:, 25]], tbl_26[ids[:, 26]], tbl_27[ids[:, 27]], tbl_28[ids[:, 28]], tbl_29[ids[:, 29]], tbl_30[ids[:, 30]], tbl_31[ids[:, 31]], tbl_32[ids[:, 32]], tbl_33[ids[:, 33]], tbl_34[ids[:, 34]], tbl_35[ids[:, 35]], tbl_36[ids[:, 36]], tbl_37[ids[:, 37]], tbl_38[ids[:, 38]], tbl_39[ids[:, 39]]], axis=1)
    z = _L0_rec_ref(e, L0_rec_wq0, L0_rec_wk0, L0_rec_wv0, L0_rec_cw0, L0_rec_wq1, L0_rec_wk1, L0_rec_wv1, L0_rec_cw1)
    z = z.reshape(z.shape[0], -1)
    h = jnp.concatenate([z, dense_ctx], axis=1)
    h = jnp.maximum(h @ W_top1 + b_top1, 0.0)
    h = jnp.maximum(h @ W_top2 + b_top2, 0.0)
    y = h @ W_top3
    return y

_drawn_inputs = setup_inputs


def setup_inputs(seed=0):
    import zlib

    import numpy as np

    out = dict(_drawn_inputs(seed))
    spreads = {'b_top1': (0.0, 0.1), 'b_top2': (0.0, 0.1)}
    factors = {'tbl_0': 8.0,
     'tbl_1': 8.0,
     'tbl_2': 8.0,
     'tbl_3': 8.0,
     'tbl_4': 8.0,
     'tbl_5': 8.0,
     'tbl_6': 8.0,
     'tbl_7': 8.0,
     'tbl_8': 8.0,
     'tbl_9': 8.0,
     'tbl_10': 8.0,
     'tbl_11': 8.0,
     'tbl_12': 8.0,
     'tbl_13': 8.0,
     'tbl_14': 8.0,
     'tbl_15': 8.0,
     'tbl_16': 8.0,
     'tbl_17': 8.0,
     'tbl_18': 8.0,
     'tbl_19': 8.0,
     'tbl_20': 8.0,
     'tbl_21': 8.0,
     'tbl_22': 8.0,
     'tbl_23': 8.0,
     'tbl_24': 8.0,
     'tbl_25': 8.0,
     'tbl_26': 8.0,
     'tbl_27': 8.0,
     'tbl_28': 8.0,
     'tbl_29': 8.0,
     'tbl_30': 8.0,
     'tbl_31': 8.0,
     'tbl_32': 8.0,
     'tbl_33': 8.0,
     'tbl_34': 8.0,
     'tbl_35': 8.0,
     'tbl_36': 8.0,
     'tbl_37': 8.0,
     'tbl_38': 8.0,
     'tbl_39': 8.0,
     'L0_rec_wq0': 8.0,
     'L0_rec_wk0': 8.0,
     'L0_rec_wv0': 8.0,
     'L0_rec_cw0': 8.0,
     'L0_rec_wq1': 64.0,
     'L0_rec_wk1': 64.0,
     'L0_rec_wv1': 8.0,
     'L0_rec_cw1': 8.0}
    for name, (base, spread) in spreads.items():
        noise = np.random.default_rng([zlib.crc32(name.encode()), seed]).standard_normal(out[name].shape)
        drawn = base * np.exp(spread * noise) if base else spread * noise
        out[name] = jnp.asarray(drawn.astype(out[name].dtype))
    for name, factor in factors.items():
        out[name] = (out[name] * factor).astype(out[name].dtype)
    return out
```

```python
from contextlib import ExitStack

import concourse.bass as bass
from concourse import mybir

F32 = mybir.dt.float32
BF16 = mybir.dt.bfloat16
I32 = mybir.dt.int32
ALU = mybir.AluOpType
ACT = mybir.ActivationFunctionType
AX = mybir.AxisListType

P = 128
B = 512
F = 40
K = 32
J = 200
G = J
CH = B // P
Q = 4
STEPS = P // Q
KH = 2
KL = K // KH
F8 = 8
FG = F // F8
U = Q * KH
NPAIR = KH * FG * Q // 2
GRP = KH * FG
C0 = F * F
CT = (C0 + P - 1) // P
XG = 4
XGS = [range(0, 4), range(4, 7), range(7, 10), range(10, CT)]
TG = len(XGS)
GT = 3
GP = (G + GT - 1) // GT
R1 = GT * F
NRND = (FG + 1) // 2
TERMS = 8
A_OF = [0, 1, 2, 0, 1, 0]
T_OF = [0, 0, 0, 1, 1, 2, 3, 4]
NT = 5
H1 = 512
H2 = 256
DD = 16
ZC = [(0, 0, P), (1, P, J - P)]
BANKS = 3
CW = {"a": 0, "q": 1, "v": 2, "a1": 3, "v1": 4}
KA = 5
KB = 5
KPL = 4
PIECE = 17


def dlrm_cin_tower(nc, dense_t, ids, tables, w_k, wq1_t, cw0, cw1, w1, b1, w2, b2, w3,
                   ident_c, zsel_c, rsel_c, diag_c, f8sel_c, onesq_c, y):
    scr_t = nc.dram_tensor("scr_t", (2, P, NT, G), BF16, kind="Internal").ap()
    scr_a = nc.dram_tensor("scr_a", (P, 3, STEPS * F), BF16, kind="Internal").ap()
    scr_v = nc.dram_tensor("scr_v", (P, F * STEPS), F32, kind="Internal").ap()
    scr_s = nc.dram_tensor("scr_s", (CH, R1, P, GP), F32, kind="Internal").ap()

    with ExitStack() as ctx:
        z0_t = ctx.enter_context(nc.sbuf_tensor("z0_t", [P, 2, B], F32))
        z1_t = ctx.enter_context(nc.sbuf_tensor("z1_t", [P, 2, B], F32))
        cin_pipeline(nc, ids, tables, w_k, wq1_t, cw0, ident_c, zsel_c, rsel_c, diag_c, f8sel_c, onesq_c,
                     scr_t, scr_a, scr_v, scr_s, z0_t)
        dense_layers(nc, dense_t, cw1, w1, b1, w2, b2, w3, ident_c, scr_s, z0_t, z1_t, y)


def cin_pipeline(nc, ids, tables, w_k, wq1_t, cw0, ident_c, zsel_c, rsel_c, diag_c, f8sel_c, onesq_c,
                 scr_t, scr_a, scr_v, scr_s, z0_t):
    with ExitStack() as ctx:
        def sb(name, shape, dt=F32):
            return ctx.enter_context(nc.sbuf_tensor(name, shape, dt))

        def psum(name):
            return ctx.enter_context(nc.psum_tensor(name, [P, 512], F32))

        def sem(name):
            return ctx.enter_context(nc.semaphore(name))

        ident = sb("ident", [P, P])
        zsel = sb("zsel", [P, KH, K])
        rsel = sb("rsel", [P, U, P])
        diag = sb("diag", [P, KL, F8], BF16)
        f8sel = sb("f8sel", [P, F8])
        onesq = sb("onesq", [P, Q])
        wk = sb("wk", [P, 5, F])
        wq1 = sb("wq1", [P, G])
        cw0_sb = sb("cw0_sb", [P, CT, J])
        ids_sb = sb("ids_sb", [P, F], I32)
        emb = sb("emb", [P, F * K])
        a0 = sb("a0", [P, STEPS, F])
        q0 = sb("q0", [P, STEPS, F])
        v0 = sb("v0", [P, STEPS, F])
        m0 = sb("m0", [P, STEPS, F])
        ext = sb("ext", [P, 4, STEPS])
        a_terms = sb("a_terms", [P, U, STEPS, F], BF16)
        vrow = sb("vrow", [P, U * FG, STEPS])
        prob = [sb(f"prob{i}", [P, F, F]) for i in range(2)]
        zr0 = sb("zr0", [P, 2, F])
        xt = sb("xt", [P, 2, XG * P])
        out0 = sb("out0", [P, J])
        t_f = sb("t_f", [P, G])
        t_d = sb("t_d", [P, G])
        m_u = sb("m_u", [P, G])
        m_f = sb("m_f", [P, G])
        t_split = sb("t_split", [P, NT, G], BF16)
        t_rows = [sb(f"t_rows{i}", [P, U, G], BF16) for i in range(2)]
        a_diag = sb("a_diag", [P, KH, Q, FG, KL * F8], BF16)
        ex = [sb(f"ex{i}", [P, GRP, Q, G]) for i in range(2)]
        rz = sb("rz", [P, G])
        vst = [sb(f"vst{i}", [P, U * FG, F8]) for i in range(2)]
        s_st = sb("s_st", [P, GT, FG, GP])
        flat = [e[:].rearrange("p a b c -> p (a b c)") for e in ex]
        SF = STEPS * F
        emb_k = flat[0][:, 0:SF]
        a1_f = flat[0][:, SF:2 * SF]
        m_tmp = flat[0][:, 2 * SF:3 * SF]
        v1_k = flat[1][:, 0:SF]
        a_split = flat[1][:, SF:SF + 3 * SF // 2].bitcast(BF16).rearrange("p (t n) -> p t n", t=3)

        ps_phi = [psum(f"ps_phi{i}") for i in range(BANKS)]
        ps_z = psum("ps_z")
        ps_r = psum("ps_r")
        ps_s = psum("ps_s")
        ps_x = psum("ps_x")
        ps_o = psum("ps_o")

        consts_in = sem("consts_in")
        cleared = sem("cleared")
        ids_in = sem("ids_in")
        emb_in = sem("emb_in")
        prep_seq = sem("prep_seq")
        a_out = sem("a_out")
        a_in = sem("a_in")
        v_out = sem("v_out")
        v_in = sem("v_in")
        prod_ready = sem("prod_ready")
        a_seq = sem("a_seq")
        l0_exp = sem("l0_exp")
        xt_ps = sem("xt_ps")
        xt_sb = sem("xt_sb")
        main_done = sem("main_done")
        out0_ready = sem("out0_ready")
        z0_ps = sem("z0_ps")
        z0_sb = sem("z0_sb")
        b_seq = sem("b_seq")
        split_seq = sem("split_seq")
        t_out = sem("t_out")
        t_in = [sem(f"t_in{i}") for i in range(2)]
        diag_ready = sem("diag_ready")
        phi_ready = sem("phi_ready")
        ex_ready = sem("ex_ready")
        z_ready = sem("z_ready")
        rz_ready = sem("rz_ready")
        rrep_ready = sem("rrep_ready")
        norm_done = sem("norm_done")
        vst_ready = sem("vst_ready")
        s_ps = sem("s_ps")
        s_sb = sem("s_sb")
        s_out = sem("s_out")
        pool_turn = sem("pool_turn")
        sp_turn = sem("sp_turn")

        block = ctx.enter_context(nc.Block())

        def pipeline(eng, prepare, tick):
            with eng.Fori(0, CH) as c:
                prepare(c)
                for t in range(-3, 1):
                    tick(c, t, t % 2)
                with eng.Fori(0, (STEPS - 4) // 2) as it:
                    tick(c, it * 2 + 1, 1)
                    tick(c, it * 2 + 2, 0)
                for t in range(STEPS - 3, STEPS + 1):
                    tick(c, t, t % 2)

        def on(b):
            return not isinstance(b, int) or 0 <= b < STEPS

        def after(c, b, per, more):
            return chunks(c, STEPS * per, b * per + more)

        def chunks(c, per, more=0):
            return c * per + (more + 1)

        def start_at_one(eng, *sems):
            for s in sems:
                eng.sem_inc(s, 1)

        def at(b):
            return bass.ds(b, 1)

        @block.sync
        def _(sp):
            start_at_one(sp, a_out, v_out, a_in, v_in, t_out, t_in[0], t_in[1], s_out)
            for q in range(Q):
                sp.dma_start(wk[K * q:K * q + K], w_k).then_inc(consts_in, 16)
                sp.dma_start(wq1[K * q:K * q + K], wq1_t).then_inc(consts_in, 16)
            for dst, src in ((ident, ident_c), (zsel, zsel_c), (rsel, rsel_c), (diag, diag_c), (f8sel, f8sel_c),
                             (onesq, onesq_c), (cw0_sb, cw0)):
                sp.dma_start(dst[:], src).then_inc(consts_in, 16)

            def prepare(c):
                sp.wait_ge(prep_seq, chunks(c, 17, 17))
                sp.dma_start(scr_a, a_split).then_inc(a_out, 16)
                sp.dma_start(scr_v, v1_k).then_inc(v_out, 16)
                sp.wait_ge(a_out, chunks(c, 16, 16))
                sp.sem_inc(sp_turn, 1)
                sp.wait_ge(diag_ready, chunks(c, STEPS * 2))
                sp.sem_inc(sp_turn, 1)
                for m, a in enumerate(A_OF):
                    sp.dma_start(a_terms[KL * m:KL * m + KL].rearrange("k u s f -> k u (s f)"),
                                 scr_a[:, a].rearrange("(u k) n -> k u n", k=KL)).then_inc(a_in, 16)
                sp.wait_ge(v_out, chunks(c, 16, 16))
                sp.sem_inc(sp_turn, 1)
                sp.wait_ge(vst_ready, chunks(c, STEPS))
                sp.dma_start(vrow[:].rearrange("p (u n) s -> p u (n s)", u=U),
                             scr_v.rearrange("(u k) (e n) -> (k e) u n", u=U, e=F8)).then_inc(v_in, 16)

            def tick(c, t, par):
                b = t - 1
                if on(b):
                    sp.wait_ge(s_sb, after(c, b, NRND, NRND))
                    sp.sem_inc(sp_turn, 1)
                    for q in range(Q):
                        src = s_st[K * q:K * q + F8].rearrange("e t g n -> e (t g) n")
                        dst = scr_s[at(c), :, bass.ds(b + K * q, 1)].rearrange("o (x e) b g -> e (o x) (b g)", e=F8)
                        sp.dma_start(dst, src).then_inc(s_out, 16)
                b = t + 2
                if on(b):
                    sp.wait_ge(b_seq, after(c, b, KB, KB))
                    sp.sem_inc(sp_turn, 1)
                    sp.wait_ge(split_seq, after(c, b, KPL, KPL))
                    sp.dma_start(scr_t[par], t_split[:]).then_inc(t_out, 16)
                    sp.wait_ge(t_out, after(c, b, 16, 16))
                    sp.sem_inc(sp_turn, 1)
                    if not isinstance(b, int) or b >= 2:
                        sp.wait_ge(phi_ready, after(c, b, NPAIR, -NPAIR))
                        sp.sem_inc(sp_turn, 1)
                    for m, s in enumerate(T_OF):
                        sp.dma_start(t_rows[par][KL * m:KL * m + KL],
                                     scr_t[par, :, s].rearrange("(u k) g -> k u g", k=KL)).then_inc(t_in[par], 16)

            pipeline(sp, prepare, tick)
            sp.wait_ge(s_out, CH * STEPS * 16 * Q + 1)

        @block.gpsimd
        def _(pool):
            start_at_one(pool, prod_ready, vst_ready, split_seq)
            pool.wait_ge(consts_in, 16 * 15)

            def prepare(c):
                pool.dma_start(ids_sb[:], ids[at(c)].rearrange("o p f -> (o p) f")).then_inc(ids_in, 16)
                pool.wait_ge(ids_in, c * 16 + 16)
                pool.wait_ge(prep_seq, chunks(c, 17))
                pool.sem_inc(pool_turn, 1)
                for f in range(F):
                    nc.gpsimd.indirect_dma_start(
                        out=emb[:, f * K:f * K + K], out_offset=None, in_=tables[f],
                        in_offset=bass.IndirectOffsetOnAxis(ap=ids_sb[:, f:f + 1], axis=0)).then_inc(emb_in, 16)
                pool.wait_ge(prep_seq, chunks(c, 17, 17))
                pool.wait_ge(v_in, chunks(c, 16, 16))

            def tick(c, t, par):
                b = t + 3
                if on(b):
                    if not isinstance(b, int) or b >= 2:
                        pool.wait_ge(xt_ps, after(c, b, TG, -TG))
                    nc.gpsimd.tensor_tensor(prob[1 - par][:],
                                            a0[:, at(b)].rearrange("p o f -> p (o f)").unsqueeze(2).to_broadcast([P, F, F]),
                                            q0[:, at(b)].to_broadcast([P, F, F]),
                                            ALU.mult).then_inc(prod_ready, 1)
                b = t
                if on(b):
                    if not isinstance(b, int) or b >= 2:
                        pool.wait_ge(s_ps, after(c, b, NRND, -NRND))
                    nc.gpsimd.tensor_tensor(vst[par][:],
                                            vrow[:, :, at(b)].to_broadcast([P, U * FG, F8]),
                                            f8sel[:].unsqueeze(1).to_broadcast([P, U * FG, F8]),
                                            ALU.mult).then_inc(vst_ready, 1)
                b = t + 2
                if on(b):
                    pool.wait_ge(b_seq, after(c, b, KB, 1))
                    pool.wait_ge(t_out, after(c, b, 16, 0))
                    pool.sem_inc(pool_turn, 1)
                    nc.gpsimd.tensor_copy(t_split[:, 0], t_f[:]).then_inc(split_seq, 1)
                    pool.wait_ge(split_seq, after(c, b, KPL, 1))
                    nc.gpsimd.tensor_tensor(t_d[:], t_f[:], t_split[:, 0], ALU.subtract).then_inc(split_seq, 1)
                    pool.wait_ge(split_seq, after(c, b, KPL, 2))
                    pool.sem_inc(pool_turn, 1)
                    nc.gpsimd.tensor_copy(t_split[:, 1], t_d[:]).then_inc(split_seq, 1)
                    pool.wait_ge(split_seq, after(c, b, KPL, 3))
                    nc.gpsimd.tensor_tensor(t_split[:, 2], t_d[:], t_split[:, 1], ALU.subtract).then_inc(split_seq, 1)

            pipeline(pool, prepare, tick)

        @block.vector
        def _(dve):
            start_at_one(dve, prep_seq, a_seq, b_seq, diag_ready, rz_ready, norm_done)
            dve.memset(a_terms[6 * KL:P].rearrange("p u s f -> p (u s f)"), -1.0).then_inc(cleared, 1)
            dve.memset(ps_s[:], 0.0).then_inc(cleared, 1)
            dve.memset(ps_o[:], 0.0).then_inc(cleared, 1)
            dve.wait_ge(consts_in, 16 * 15)

            def prepare(c):
                done = [0]

                def then(ins):
                    done[0] += 1
                    ins.then_inc(prep_seq, 1)

                def prior():
                    dve.wait_ge(prep_seq, chunks(c, 17, done[0]))

                def w(name):
                    return wk[:, CW[name]]

                def over_steps(x):
                    return x.unsqueeze(1).to_broadcast([P, STEPS, F])

                dve.wait_ge(emb_in, c * (16 * F) + 16 * F)
                dve.wait_ge(s_ps, chunks(c, STEPS * NRND))
                then(nc.vector.transpose(emb_k, emb[:]))
                prior()
                fb = emb_k.rearrange("p (f s) -> p s f", f=F)
                then(nc.vector.tensor_tensor(a0[:], fb, over_steps(w("a")), ALU.mult))
                then(nc.vector.tensor_tensor(q0[:], fb, over_steps(w("q")), ALU.mult))
                then(nc.vector.tensor_tensor(v0[:], fb, over_steps(w("v")), ALU.mult))
                then(nc.vector.tensor_tensor(
                    a1_f.rearrange("p (s g e) -> p s g e", s=STEPS, g=FG),
                    emb_k.rearrange("p (e g s) -> p s g e", e=F8, g=FG),
                    w("a1").rearrange("p (e g) -> p g e", e=F8).unsqueeze(1).to_broadcast([P, STEPS, FG, F8]), ALU.mult))
                then(nc.vector.tensor_tensor(
                    v1_k.rearrange("p (f s) -> p f s", f=F), emb_k.rearrange("p (f s) -> p f s", f=F),
                    w("v1").unsqueeze(2).to_broadcast([P, F, STEPS]), ALU.mult))
                prior()
                a1 = a1_f.rearrange("p (s f) -> p s f", f=F)
                then(nc.vector.tensor_reduce(ext[:, 0], a0[:], AX.X, ALU.max))
                then(nc.vector.tensor_reduce(ext[:, 1], a0[:], AX.X, ALU.min))
                then(nc.vector.tensor_reduce(ext[:, 2], a1, AX.X, ALU.max))
                then(nc.vector.tensor_reduce(ext[:, 3], a1, AX.X, ALU.min))
                prior()
                tmp = m_tmp.rearrange("p (s f) -> p s f", f=F)
                then(nc.vector.tensor_tensor(tmp, q0[:], ext[:, 0].unsqueeze(2).to_broadcast([P, STEPS, F]), ALU.mult))
                then(nc.vector.tensor_tensor(m0[:], q0[:], ext[:, 1].unsqueeze(2).to_broadcast([P, STEPS, F]), ALU.mult))
                then(nc.vector.tensor_copy(a_split[:, 0], a1_f))
                prior()
                then(nc.vector.tensor_tensor(m0[:], m0[:], tmp, ALU.max))
                then(nc.vector.tensor_tensor(a1_f, a1_f, a_split[:, 0], ALU.subtract))
                prior()
                then(nc.vector.tensor_copy(a_split[:, 1], a1_f))
                prior()
                then(nc.vector.tensor_tensor(a_split[:, 2], a1_f, a_split[:, 1], ALU.subtract))
                prior()
                assert done[0] == 17
                dve.wait_ge(a_in, chunks(c, 16 * 6, 16 * 6))
                dve.wait_ge(cleared, 3)
                make_diag(c, 0, 0)
                make_diag(c, 0, 1)

            def make_diag(c, b, kh):
                if not (isinstance(b, int) and b == 0):
                    dve.wait_ge(phi_ready, after(c, b, NPAIR, -NPAIR + NPAIR // KH * (kh + 1)))
                mask = diag[:].unsqueeze(1).to_broadcast([P, FG, KL, F8])
                for q in range(Q):
                    src = a_terms[:, q * KH + kh, at(b)].rearrange("p o (g e) -> p (o g) e", e=F8)
                    last = nc.vector.tensor_tensor(a_diag[:, kh, q].rearrange("p g (k e) -> p g k e", e=F8), mask,
                                                   src.unsqueeze(2).to_broadcast([P, FG, KL, F8]), ALU.mult)
                last.then_inc(diag_ready, 1)

            def tick(c, t, par):
                m, a, l, d = t - 1, t + 3, t + 2, t + 1

                def normalise(r):
                    if not on(m):
                        return
                    kh, qh = divmod(r, 2)
                    dve.wait_ge(rrep_ready, after(c, m, 4, r + 1))
                    e = ex[1 - par][:, kh * FG:kh * FG + FG, 2 * qh:2 * qh + 2, :].rearrange("p g q n -> p g (q n)")
                    nc.vector.tensor_tensor(e, e, ps_r[:, 0:2 * G].unsqueeze(1).to_broadcast([P, FG, 2 * G]),
                                            ALU.mult).then_inc(norm_done, 1)

                if on(m):
                    dve.wait_ge(z_ready, after(c, m, 1, 1))
                    dve.wait_ge(rrep_ready, after(c, m, 4, 0))
                    nc.vector.reciprocal(rz[:], ps_z[:, 0:G]).then_inc(rz_ready, 1)
                normalise(0)
                x = prob[1 - par]
                if on(a):
                    dve.wait_ge(prod_ready, after(c, a, 1, 1))
                    nc.vector.tensor_tensor(x[:], x[:], m0[:, at(a)].to_broadcast([P, F, F]),
                                            ALU.subtract).then_inc(a_seq, 1)
                normalise(1)
                normalise(2)
                normalise(3)
                if on(d) and d is not 0:
                    make_diag(c, d, 0)
                if on(a):
                    dve.wait_ge(l0_exp, after(c, a, 1, 1))
                    nc.vector.tensor_reduce(zr0[:, 0], x[:].rearrange("p f g -> p g f"), AX.X, ALU.add).then_inc(a_seq, 1)
                    dve.wait_ge(a_seq, after(c, a, KA, 2))
                    nc.vector.reciprocal(zr0[:, 1], zr0[:, 0]).then_inc(a_seq, 1)
                    dve.wait_ge(a_seq, after(c, a, KA, 3))
                    nc.vector.tensor_tensor(x[:], x[:], zr0[:, 1].unsqueeze(1).to_broadcast([P, F, F]),
                                            ALU.mult).then_inc(a_seq, 1)
                    dve.wait_ge(a_seq, after(c, a, KA, 4))
                    nc.vector.tensor_tensor(x[:], x[:],
                                            v0[:, at(a)].rearrange("p o f -> p (o f)").unsqueeze(2).to_broadcast([P, F, F]),
                                            ALU.mult).then_inc(a_seq, 1)
                if on(l):
                    dve.wait_ge(out0_ready, after(c, l, 1, 1))
                    dve.wait_ge(split_seq, after(c, l, KPL, 0))
                    nc.vector.tensor_tensor(t_f[:], out0[:], wq1[:], ALU.mult).then_inc(b_seq, 1)
                    dve.wait_ge(b_seq, after(c, l, KB, 1))
                    nc.vector.tensor_scalar(m_u[:], t_f[:], ext[:, 2, at(l)], None, ALU.mult).then_inc(b_seq, 1)
                    dve.wait_ge(b_seq, after(c, l, KB, 2))
                    nc.vector.scalar_tensor_tensor(out=m_f[:], in0=t_f[:], scalar=ext[:, 3, at(l)], in1=m_u[:],
                                                   op0=ALU.mult, op1=ALU.max).then_inc(b_seq, 1)
                    dve.wait_ge(b_seq, after(c, l, KB, 3))
                    dve.wait_ge(t_out, after(c, l, 16, 0))
                    nc.vector.tensor_copy(t_split[:, 3], m_f[:]).then_inc(b_seq, 1)
                    dve.wait_ge(b_seq, after(c, l, KB, 4))
                    nc.vector.tensor_tensor(t_split[:, 4], m_f[:], t_split[:, 3], ALU.subtract).then_inc(b_seq, 1)
                if on(d) and d is not 0:
                    make_diag(c, d, 1)

            pipeline(dve, prepare, tick)

        @block.scalar
        def _(act):
            start_at_one(act, l0_exp, xt_sb, out0_ready, z0_sb, ex_ready, s_sb)
            act.wait_ge(cleared, 3)

            def tick(c, t, par):
                n, m, a, l = t, t - 1, t + 3, t + 2

                def sums(rnd):
                    w = min(2, FG - 2 * rnd)
                    act.wait_ge(s_ps, after(c, m, NRND, rnd + 1))
                    if rnd == 0:
                        act.wait_ge(s_out, after(c, m, 16 * Q, 0))
                    nc.scalar.copy(s_st[:].rearrange("p t g n -> p g t n")[:, 2 * rnd:2 * rnd + w],
                                   ps_s[:].rearrange("p (g x) -> p g x", g=2)[:, 0:w, 0:GT * GP]
                                   .rearrange("p g (t n) -> p g t n", t=GT)).then_inc(s_sb, 1)

                for j in range(GRP):
                    if on(n):
                        for p in (2 * j, 2 * j + 1):
                            if p == 0 and (not isinstance(n, int) or n >= 2):
                                act.wait_ge(s_ps, after(c, n, NRND, -NRND))
                            act.wait_ge(phi_ready, after(c, n, NPAIR, p + 1))
                            qh = p % 2
                            nc.scalar.activation(
                                ex[par][:, j, 2 * qh:2 * qh + 2, :].rearrange("p q g -> p (q g)"),
                                ps_phi[p % BANKS][:, 0:2 * G], ACT.Exp).then_inc(ex_ready, 1)
                    if on(l) and j < TG:
                        act.wait_ge(xt_ps, after(c, l, TG, j + 1))
                        if not (isinstance(l, int) and l == 0 and j < 2):
                            act.wait_ge(main_done, after(c, l, TG, j - 1))
                        cols = P * (len(XGS[j]) - (j == TG - 1))
                        ins = nc.scalar.copy(xt[:, j % 2, 0:cols], ps_x[:, 0:cols])
                        if j == TG - 1:
                            rows = C0 - (CT - 1) * P
                            ins = nc.scalar.copy(xt[0:rows, j % 2, cols:cols + P], ps_x[0:rows, cols:cols + P])
                        ins.then_inc(xt_sb, 1)
                    if on(a) and j == 3:
                        act.wait_ge(a_seq, after(c, a, KA, 1))
                        x = prob[1 - par][:].rearrange("p f g -> p (f g)")
                        nc.scalar.activation(x, x, ACT.Exp).then_inc(l0_exp, 1)
                    if on(l) and j == 5:
                        act.wait_ge(main_done, after(c, l, TG, TG))
                        act.wait_ge(z0_ps, after(c, l, 1, 0))
                        act.wait_ge(b_seq, after(c, l, KB, 0))
                        nc.scalar.copy(out0[:], ps_o[:, 0:J]).then_inc(out0_ready, 1)
                    if on(l) and j == 8:
                        act.wait_ge(z0_ps, after(c, l, 1, 1))
                        dst = z0_t[:].rearrange("p h (c q s) -> p h c q s", c=CH, q=Q)
                        dst = dst[:, :, at(c), :, at(l)].rearrange("p h o q s -> p h (o q s)")
                        nc.scalar.copy(dst, ps_o[:, 256:256 + 2 * Q].rearrange("p (h q) -> p h q", h=2)).then_inc(z0_sb, 1)
                    if on(m) and j in (7, 9):
                        sums((j - 7) // 2)
                if on(m):
                    sums(2)

            pipeline(act, lambda c: None, tick)

        @block.tensor
        def _(pe):
            start_at_one(pe, xt_ps, main_done, z0_ps, phi_ready, z_ready, rrep_ready, s_ps)
            pe.wait_ge(consts_in, 16 * 15)
            pe.wait_ge(cleared, 3)

            def tick(c, t, par):
                n, m, l = t, t - 1, t + 2

                def logits(p):
                    j, qh = divmod(p, 2)
                    kh, fg = divmod(j, FG)
                    if p == 0:
                        half = 16 * TERMS // 2
                        pe.wait_ge(t_in[par], after(c, n, half, 2 * half - half * par))
                    if qh == 0 and fg == 0:
                        pe.wait_ge(diag_ready, after(c, n, 2, kh + 1))
                    last = p - BANKS if p >= BANKS else max(x for x in range(NPAIR) if x % BANKS == p) - NPAIR
                    if last >= 0 or not (isinstance(n, int) and n == 0):
                        pe.wait_ge(ex_ready, after(c, n, NPAIR, last + 1))
                    for i in range(2):
                        q = 2 * qh + i
                        mm = nc.tensor.matmul(ps_phi[p % BANKS][:, i * G:i * G + G], a_diag[:, kh, q, fg, :],
                                              t_rows[par][:, q * KH + kh, :], start=True, stop=True)
                    mm.then_inc(phi_ready, 1)

                def sum_f(j):
                    pe.wait_ge(ex_ready, after(c, n, NPAIR, 2 * j + 2))
                    if j == 0:
                        pe.wait_ge(rz_ready, after(c, n, 1, 0))
                    for q in range(Q):
                        mm = nc.tensor.matmul(ps_z[K * q:K * q + K, 0:G], zsel[:, j // FG, :], ex[par][:, j, q, :],
                                              start=(j == 0), stop=(j == GRP - 1))
                    if j == GRP - 1:
                        mm.then_inc(z_ready, 1)

                def spread(r):
                    kh, qh = divmod(r, 2)
                    if r == 0:
                        pe.wait_ge(rz_ready, after(c, m, 1, 1))
                    pe.wait_ge(norm_done, after(c, m, 4, r))
                    for i in range(2):
                        mm = nc.tensor.matmul(ps_r[:, i * G:i * G + G], rsel[:, (2 * qh + i) * KH + kh, :], rz[:],
                                              start=True, stop=True)
                    mm.then_inc(rrep_ready, 1)

                def sum_k(rnd):
                    if rnd == 0:
                        pe.wait_ge(norm_done, after(c, m, 4, 4))
                        pe.wait_ge(vst_ready, after(c, m, 1, 1))
                    pe.wait_ge(s_sb, after(c, m, NRND, rnd))
                    for fg in range(2 * rnd, min(2 * rnd + 2, FG)):
                        for kh in range(KH):
                            for q in range(Q):
                                mm = nc.tensor.matmul(
                                    ps_s[K * q:K * q + F8, 256 * (fg % 2):256 * (fg % 2) + G],
                                    vst[1 - par][:, (q * KH + kh) * FG + fg, :], ex[1 - par][:, kh * FG + fg, q, :],
                                    start=(kh == 0), stop=(kh == KH - 1))
                    mm.then_inc(s_ps, 1)

                def turn(g):
                    if g == 0:
                        pe.wait_ge(a_seq, after(c, l, KA, KA))
                    pe.wait_ge(xt_sb, after(c, l, TG, g))
                    x = prob[par][:].rearrange("p f g -> p (f g)")
                    for i, ct in enumerate(XGS[g]):
                        w = min(P, C0 - ct * P)
                        mm = nc.tensor.transpose(ps_x[0:w, i * P:i * P + P], x[:, ct * P:ct * P + w], ident[:])
                    mm.then_inc(xt_ps, 1)

                def layer1(g):
                    pe.wait_ge(xt_sb, after(c, l, TG, g + 1))
                    if g == 0:
                        pe.wait_ge(z0_sb, after(c, l, 1, 0))
                    for i, ct in enumerate(XGS[g]):
                        w = min(P, C0 - ct * P)
                        mm = nc.tensor.matmul(ps_o[:, 0:J], xt[0:w, g % 2, i * P:i * P + P], cw0_sb[0:w, ct, :],
                                              start=(ct == 0), stop=(ct == CT - 1))
                    mm.then_inc(main_done, 1)

                for j in range(GRP):
                    if on(n):
                        logits(2 * j)
                        logits(2 * j + 1)
                        if j:
                            sum_f(j - 1)
                    if on(m) and j < 4:
                        spread(j)
                    if on(l):
                        if j < TG:
                            turn(j)
                        if 1 <= j <= TG:
                            layer1(j - 1)
                        if j == 7:
                            pe.wait_ge(out0_ready, after(c, l, 1, 1))
                            for h, j0, w in ZC:
                                mm = nc.tensor.matmul(ps_o[0:w, 256 + Q * h:256 + Q * h + Q], out0[:, j0:j0 + w],
                                                      onesq[:], start=True, stop=True)
                            mm.then_inc(z0_ps, 1)
                    if on(m) and j in (6, 8):
                        sum_k((j - 6) // 2)
                if on(n):
                    sum_f(GRP - 1)
                if on(m):
                    sum_k(2)

            pipeline(pe, lambda c: None, tick)


def dense_layers(nc, dense_t, cw1, w1, b1, w2, b2, w3, ident_c, scr_s, z0_t, z1_t, y):
    n1, n2 = H1 // P, H2 // P
    z_rows = [(0, z0_t, 0, P), (1, z0_t, 1, J - P), (2, z1_t, 0, P), (3, z1_t, 1, J - P)]
    n_w = 9
    with ExitStack() as ctx:
        def sb(name, shape, dt=F32):
            return ctx.enter_context(nc.sbuf_tensor(name, shape, dt))

        def psum(name):
            return ctx.enter_context(nc.psum_tensor(name, [P, 512], F32))

        def sem(name):
            return ctx.enter_context(nc.semaphore(name))

        cw1_sb = sb("cw1_sb", [R1, GP, J])
        s_rows = [sb(f"s_rows{i}", [R1, P, GP]) for i in range(2)]
        w1_sb = sb("w1_sb", [P, 5, H1])
        w2_sb = sb("w2_sb", [P, n1, H2])
        w3_sb = sb("w3_sb", [P, n2])
        b1_sb = sb("b1_sb", [P, n1])
        b2_sb = sb("b2_sb", [P, n2])
        dense_sb = sb("dense_sb", [DD, B])
        ident = sb("ident2", [P, P])
        z1_b = sb("z1_b", [P, J])
        h1 = sb("h1", [P, n1, B])
        h2 = sb("h2", [P, n2, B])
        y_sb = sb("y_sb", [1, B])
        ps_z1 = psum("ps_z1")
        ps_t = psum("ps_t")
        ps_h = [psum(f"ps_h{i}") for i in range(4)]

        cw1_in = [sem(f"cw1_in{i}") for i in range((GP + PIECE - 1) // PIECE)]
        srow_in = [sem(f"srow_in{i}") for i in range(2)]
        weights_in = sem("weights_in")
        z1_ps = sem("z1_ps")
        z1_sb = sem("z1_sb")
        z1t_ps = sem("z1t_ps")
        z1t_sb = sem("z1t_sb")
        h_ps = sem("h_ps")
        h_sb = sem("h_sb")
        y_out = sem("y_out")

        block = ctx.enter_context(nc.Block())

        @block.sync
        def _(sp):
            sp.dma_start(s_rows[0][:], scr_s[0]).then_inc(srow_in[0], 16)
            for g in range(0, GP, PIECE):
                w = min(PIECE, GP - g)
                sp.dma_start(cw1_sb[:, g:g + w], cw1[:, g:g + w]).then_inc(cw1_in[g // PIECE], 16)
            sp.dma_start(s_rows[1][:], scr_s[1]).then_inc(srow_in[1], 16)
            sp.dma_start(ident[:], ident_c).then_inc(weights_in, 16)
            for i, r0, rows in ((0, 0, P), (1, P, J - P), (2, J, P), (3, J + P, J - P), (4, 2 * J, DD)):
                sp.dma_start(w1_sb[0:rows, i], w1[r0:r0 + rows]).then_inc(weights_in, 16)
            for dst, src in ((w2_sb, w2), (w3_sb, w3), (b1_sb, b1), (b2_sb, b2), (dense_sb, dense_t)):
                sp.dma_start(dst[:], src).then_inc(weights_in, 16)
            for c in range(2, CH):
                sp.wait_ge(z1_ps, c - 1)
                sp.dma_start(s_rows[c % 2][:], scr_s[c]).then_inc(srow_in[c % 2], 16)
            sp.wait_ge(h_sb, n1 + n2 + 1)
            sp.dma_start(y, y_sb[:]).then_inc(y_out, 16)
            sp.wait_ge(y_out, 16)

        @block.tensor
        def _(pe):
            pe.sem_inc(z1t_ps, 1)

            def turn(c):
                pe.wait_ge(z1_sb, c + 2)
                pe.wait_ge(weights_in, 16 * 11)
                pe.wait_ge(z1t_sb, c + 1)
                for h, j0, w in ZC:
                    mm = nc.tensor.transpose(ps_t[0:w, h * P:h * P + P], z1_b[:, j0:j0 + w], ident[:])
                mm.then_inc(z1t_ps, 1)

            with pe.Fori(0, CH // 2) as pair:
                for i in range(2):
                    c = pair * 2 + i
                    pe.wait_ge(srow_in[i], pair * 16 + 16)
                    pe.wait_ge(z1_sb, c + 1)
                    for g in range(GP):
                        if g % PIECE == 0:
                            pe.wait_ge(cw1_in[g // PIECE], 16)
                        mm = nc.tensor.matmul(ps_z1[:, 0:J], s_rows[i][:, :, g], cw1_sb[:, g, :],
                                              start=(g == 0), stop=(g == GP - 1))
                    mm.then_inc(z1_ps, 1)
                    turn(c)
            pe.wait_ge(z1t_sb, CH + 1)
            for m in range(n1):
                for i, z, h, rows in z_rows:
                    nc.tensor.matmul(ps_h[m % 4][:], w1_sb[0:rows, i, m * P:m * P + P], z[0:rows, h, :],
                                     start=(i == 0), stop=False)
                nc.tensor.matmul(ps_h[m % 4][:], w1_sb[0:DD, 4, m * P:m * P + P], dense_sb[:],
                                 start=False, stop=True).then_inc(h_ps, 1)
            pe.wait_ge(h_sb, n1)
            for m in range(n2):
                for i in range(n1):
                    mm = nc.tensor.matmul(ps_h[m][:], w2_sb[:, i, m * P:m * P + P], h1[:, i, :],
                                          start=(i == 0), stop=(i == n1 - 1))
                mm.then_inc(h_ps, 1)
            pe.wait_ge(h_sb, n1 + n2)
            for m in range(n2):
                mm = nc.tensor.matmul(ps_h[2][0:1, :], w3_sb[:, m:m + 1], h2[:, m, :], start=(m == 0), stop=(m == n2 - 1))
            mm.then_inc(h_ps, 1)

        @block.scalar
        def _(act):
            act.sem_inc(z1_sb, 1)
            act.sem_inc(z1t_sb, 1)
            with act.Fori(0, CH) as c:
                act.wait_ge(z1_ps, c + 1)
                act.wait_ge(z1t_ps, c + 1)
                nc.scalar.copy(z1_b[:], ps_z1[:, 0:J]).then_inc(z1_sb, 1)
                act.wait_ge(z1t_ps, c + 2)
                for h, j0, w in ZC:
                    ins = nc.scalar.copy(z1_t[0:w, h, bass.ds(c * P, P)], ps_t[0:w, h * P:h * P + P])
                ins.then_inc(z1t_sb, 1)
            act.wait_ge(weights_in, 16 * 11)
            for m in range(n1):
                act.wait_ge(h_ps, m + 1)
                nc.scalar.activation(h1[:, m, :], ps_h[m % 4][:], ACT.Relu, bias=b1_sb[:, m:m + 1]).then_inc(h_sb, 1)
            for m in range(n2):
                act.wait_ge(h_ps, n1 + m + 1)
                nc.scalar.activation(h2[:, m, :], ps_h[m][:], ACT.Relu, bias=b2_sb[:, m:m + 1]).then_inc(h_sb, 1)
            act.wait_ge(h_ps, n1 + n2 + 1)
            nc.scalar.copy(y_sb[:], ps_h[2][0:1, :]).then_inc(h_sb, 1)


def kernel(**inputs):
    import ml_dtypes
    import numpy as np
    import concourse.bacc as bacc
    from concourse.bass_utils import run_bass_kernel_spmd

    x = {k: np.asarray(v) for k, v in inputs.items()}
    p = np.arange(P)
    zsel = np.zeros((P, KH, K), np.float32)
    rsel = np.zeros((P, U, P), np.float32)
    for kh in range(KH):
        zsel[p, kh, kh * KL + p // F8] = 1
    for u in range(U):
        rsel[u * KL + p // F8, u, p] = 1
    diag = (p[:, None, None] % KL == np.arange(KL)[None, :, None]) * np.ones((1, 1, F8))
    f8sel = (p[:, None] % F8 == np.arange(F8)[None]) * 1.0
    onesq = (p[:, None] // K == np.arange(Q)[None]) * 1.0

    def rows(name):
        return x["L0_rec_" + name][0].T

    cw0 = np.pad(x["L0_rec_cw0"][0], ((0, CT * P - C0), (0, 0))).reshape(CT, P, J).transpose(1, 0, 2)
    cw1 = np.pad(x["L0_rec_cw1"][0].reshape(F8, FG, G, J), ((0, 0), (0, 0), (0, GT * GP - G), (0, 0)))
    cw1 = cw1.reshape(F8, FG, GT, GP, J).transpose(2, 1, 0, 3, 4).reshape(R1, GP, J)
    arrays = {
        "dense_t": x["dense_ctx"].T, "ids": x["ids"].reshape(CH, P, F),
        "w_k": np.stack([rows("wk0"), rows("wq0"), rows("wv0"), rows("wk1"), rows("wv1")], 1), "wq1_t": rows("wq1"),
        "cw0": cw0, "cw1": cw1, "w1": x["W_top1"], "b1": x["b_top1"].reshape(-1, P).T,
        "w2": x["W_top2"].reshape(-1, P, H2).transpose(1, 0, 2), "b2": x["b_top2"].reshape(-1, P).T,
        "w3": x["W_top3"].reshape(-1, P).T, "ident": np.eye(P, dtype=np.float32), "zsel": zsel, "rsel": rsel,
        "diag": diag.astype(ml_dtypes.bfloat16), "f8sel": f8sel.astype(np.float32), "onesq": onesq.astype(np.float32),
    }
    arrays.update({f"tbl_{f}": x[f"tbl_{f}"] for f in range(F)})
    arrays = {k: np.ascontiguousarray(v) for k, v in arrays.items()}
    nc = bacc.Bacc("TRN2", target_bir_lowering=False, num_devices=1)
    d = {k: nc.dram_tensor("in_" + k, v.shape, mybir.dt.from_np(v.dtype), kind="ExternalInput").ap() for k, v in arrays.items()}
    y = nc.dram_tensor("y", (1, B), F32, kind="ExternalOutput").ap()
    dlrm_cin_tower(nc, d["dense_t"], d["ids"], [d[f"tbl_{f}"] for f in range(F)], d["w_k"], d["wq1_t"], d["cw0"],
                   d["cw1"], d["w1"], d["b1"], d["w2"], d["b2"], d["w3"], d["ident"], d["zsel"], d["rsel"],
                   d["diag"], d["f8sel"], d["onesq"], y)
    r = run_bass_kernel_spmd(nc, [{"in_" + k: v for k, v in arrays.items()}], core_ids=[0])
    return r.results[0]["y"].reshape(B, 1)
```

```python
from contextlib import ExitStack

import concourse.bass as bass
from concourse import mybir

F32 = mybir.dt.float32
BF16 = mybir.dt.bfloat16
I32 = mybir.dt.int32
ALU = mybir.AluOpType
ACT = mybir.ActivationFunctionType
AX = mybir.AxisListType

P = 128
B = 512
F = 40
K = 32
J = 200
G = J
CH = B // P
Q = 4
STEPS = P // Q
KH = 2
KL = K // KH
F8 = 8
FG = F // F8
U = Q * KH
NPAIR = KH * FG * Q // 2
GRP = KH * FG
C0 = F * F
CT = (C0 + P - 1) // P
XG = 4
XGS = [range(0, 4), range(4, 7), range(7, 10), range(10, CT)]
TG = len(XGS)
GT = 3
GP = (G + GT - 1) // GT
R1 = GT * F
NRND = (FG + 1) // 2
TERMS = 8
A_OF = [0, 1, 2, 0, 1, 0]
T_OF = [0, 0, 0, 1, 1, 2, 3, 4]
NT = 5
H1 = 512
H2 = 256
DD = 16
ZC = [(0, 0, P), (1, P, J - P)]
BANKS = 2
CW = {"a": 0, "q": 1, "v": 2, "a1": 3, "v1": 4}
KA = 3
KB = 5
KD = 2
KPREP = 16
SEG = STEPS // 2
PEEL = 8
KLOGIT = 7
KPL = 4
PIECE = 17


def dlrm_cin_tower(nc, dense_t, ids, tables, w_k, wq1_t, cw0, cw1, w1, b1, w2, b2, w3,
                   ident_c, zsel_c, rsel_c, diag_c, f8sel_c, onesq_c, y):
    scr_t = nc.dram_tensor("scr_t", (2, P, NT, G), BF16, kind="Internal").ap()
    scr_a = nc.dram_tensor("scr_a", (P, 3, SEG * F), BF16, kind="Internal").ap()
    scr_v = nc.dram_tensor("scr_v", (P, F * SEG), F32, kind="Internal").ap()
    scr_s = nc.dram_tensor("scr_s", (CH, R1, P, GP), F32, kind="Internal").ap()

    with ExitStack() as ctx:
        z0_t = ctx.enter_context(nc.sbuf_tensor("z0_t", [P, 2, B], F32))
        z1_t = ctx.enter_context(nc.sbuf_tensor("z1_t", [P, 2, B], F32))
        cin_pipeline(nc, ids, tables, w_k, wq1_t, cw0, ident_c, zsel_c, rsel_c, diag_c, f8sel_c, onesq_c,
                     scr_t, scr_a, scr_v, scr_s, z0_t)
        dense_layers(nc, dense_t, cw1, w1, b1, w2, b2, w3, ident_c, scr_s, z0_t, z1_t, y)


def cin_pipeline(nc, ids, tables, w_k, wq1_t, cw0, ident_c, zsel_c, rsel_c, diag_c, f8sel_c, onesq_c,
                 scr_t, scr_a, scr_v, scr_s, z0_t):
    with ExitStack() as ctx:
        def sb(name, shape, dt=F32):
            return ctx.enter_context(nc.sbuf_tensor(name, shape, dt))

        def psum(name):
            return ctx.enter_context(nc.psum_tensor(name, [P, 512], F32))

        def sem(name):
            return ctx.enter_context(nc.semaphore(name))

        ident = sb("ident", [P, P])
        zsel = sb("zsel", [P, KH, K])
        rsel = sb("rsel", [P, U, P])
        diag = sb("diag", [P, KL, F8], BF16)
        f8sel = sb("f8sel", [P, F8])
        onesq = sb("onesq", [P, Q])
        wk = sb("wk", [P, 5, F])
        wq1 = sb("wq1", [P, G])
        cw0_sb = sb("cw0_sb", [P, CT, J])
        ids_sb = sb("ids_sb", [P, F], I32)
        emb = sb("emb", [P, F * K])
        a0 = sb("a0", [P, STEPS, F])
        q0 = sb("q0", [P, STEPS, F])
        v0 = sb("v0", [P, STEPS, F])
        m0 = sb("m0", [P, STEPS, F])
        ext = sb("ext", [P, 4, STEPS])
        a_terms = sb("a_terms", [P, U, STEPS, F], BF16)
        vrow = sb("vrow", [P, 2, U * FG, SEG])
        emb_k = sb("emb_k", [P, F, STEPS])
        a1_f = sb("a1_f", [P, SEG, F])
        m_tmp = sb("m_tmp", [P, SEG, F])
        v1_k = sb("v1_k", [P, F, SEG])
        a_split = sb("a_split", [P, 3, SEG, F], BF16)
        prob = [sb(f"prob{i}", [P, F, F]) for i in range(2)]
        zr0 = sb("zr0", [P, 2, F])
        xt = sb("xt", [P, 2, XG * P])
        out0 = sb("out0", [P, J])
        t_f = sb("t_f", [P, G])
        t_d = sb("t_d", [P, G])
        m_u = sb("m_u", [P, G])
        m_f = sb("m_f", [P, G])
        t_split = sb("t_split", [P, NT, G], BF16)
        t_rows = [sb(f"t_rows{i}", [P, U, G], BF16) for i in range(2)]
        a_diag = sb("a_diag", [P, KH, Q, FG, KL * F8], BF16)
        ex = [sb(f"ex{i}", [P, GRP, Q, G]) for i in range(2)]
        rz = sb("rz", [P, G])
        vst = [sb(f"vst{i}", [P, U * FG, F8]) for i in range(2)]
        s_st = sb("s_st", [P, GT, FG, GP])
        ps_phi = [psum(f"ps_phi{i}") for i in range(BANKS)]
        ps_z = psum("ps_z")
        ps_r = [psum(f"ps_r{i}") for i in range(2)]
        ps_s = psum("ps_s")
        ps_sums = [ps_s, ps_r[0], ps_r[1]]
        ps_x = psum("ps_x")
        ps_o = psum("ps_o")

        consts_in = sem("consts_in")
        cleared = sem("cleared")
        ids_in = sem("ids_in")
        emb_in = sem("emb_in")
        prep_seq = sem("prep_seq")
        a_out = sem("a_out")
        a_in = sem("a_in")
        v_out = sem("v_out")
        v_in = sem("v_in")
        emb_taken = sem("emb_taken")
        logit_seq = sem("logit_seq")
        x_ready = sem("x_ready")
        a_seq = sem("a_seq")
        l0_exp = sem("l0_exp")
        xt_ps = sem("xt_ps")
        xt_sb = sem("xt_sb")
        main_done = sem("main_done")
        out0_ready = sem("out0_ready")
        z0_ps = sem("z0_ps")
        z0_sb = sem("z0_sb")
        b_seq = sem("b_seq")
        split_seq = sem("split_seq")
        t_out = sem("t_out")
        t_in = [sem(f"t_in{i}") for i in range(2)]
        diag_ready = sem("diag_ready")
        phi_ready = sem("phi_ready")
        ex_ready = sem("ex_ready")
        z_ready = sem("z_ready")
        rz_ready = sem("rz_ready")
        rrep_ready = sem("rrep_ready")
        norm_done = sem("norm_done")
        vst_ready = sem("vst_ready")
        s_ps = sem("s_ps")
        s_sb = sem("s_sb")
        s_out = sem("s_out")
        pool_turn = sem("pool_turn")
        sp_turn = sem("sp_turn")

        block = ctx.enter_context(nc.Block())

        def pipeline(eng, tick):
            def segment(c, h):
                for s in range(PEEL):
                    tick(c, h, SEG * h + s - 3, (s + 1) % 2, s)
                with eng.Fori(0, (SEG - PEEL) // 2) as it:
                    tick(c, h, it * 2 + (SEG * h + PEEL - 3), 1)
                    tick(c, h, it * 2 + (SEG * h + PEEL - 2), 0)

            segment(0, 0)
            segment(0, 1)
            with eng.Fori(1, CH) as c:
                segment(c, 0)
                segment(c, 1)
            for t in range(STEPS - 3, STEPS + 1):
                tick(CH - 1, 1, t, t % 2)

        def on(c, b):
            return not (isinstance(c, int) and isinstance(b, int)) or 0 <= c * STEPS + b < B // Q

        def early(c, b, n):
            return isinstance(c, int) and isinstance(b, int) and c * STEPS + b < n

        def after(c, b, per, more):
            return chunks(c, STEPS * per, b * per + more)

        def chunks(c, per, more=0):
            return c * per + (more + 1)

        def start_at_one(eng, *sems):
            for s in sems:
                eng.sem_inc(s, 1)

        def at(b):
            return bass.ds(b % STEPS if isinstance(b, int) else b, 1)

        def chunk_of(c, b):
            return c - 1 if isinstance(b, int) and b < 0 else c

        def prepared(c, b, per):
            return chunks(c, 2 * per, (b // SEG + 1) * per)

        def next_half(c, h):
            return (c, 1) if h == 0 else (c + 1, 0)

        def half_of(b, h):
            if isinstance(b, int):
                return b % STEPS // SEG, bass.ds(b % SEG, 1)
            return h, bass.ds(b - SEG * h, 1)

        @block.sync
        def _(sp):
            start_at_one(sp, a_out, v_out, a_in, v_in, t_out, t_in[0], t_in[1], s_out)
            for q in range(Q):
                sp.dma_start(wk[K * q:K * q + K], w_k).then_inc(consts_in, 16)
                sp.dma_start(wq1[K * q:K * q + K], wq1_t).then_inc(consts_in, 16)
            for dst, src in ((ident, ident_c), (zsel, zsel_c), (rsel, rsel_c), (diag, diag_c), (f8sel, f8sel_c),
                             (onesq, onesq_c), (cw0_sb, cw0)):
                sp.dma_start(dst[:], src).then_inc(consts_in, 16)

            def store_prepared(c, h):
                half = chunks(c, 2 * 16, (h + 1) * 16)
                sp.wait_ge(prep_seq, chunks(c, 2 * KPREP, (h + 1) * KPREP))
                sp.dma_start(scr_a, a_split[:].rearrange("p t s f -> p t (s f)")).then_inc(a_out, 16)
                sp.dma_start(scr_v, v1_k[:].rearrange("p f s -> p (f s)")).then_inc(v_out, 16)
                sp.wait_ge(a_out, half)
                sp.sem_inc(sp_turn, 1)
                if not early(c, h, 2):
                    sp.wait_ge(diag_ready, after(c, SEG * (h - 1), KD, 0))
                    sp.sem_inc(sp_turn, 1)
                    sp.wait_ge(vst_ready, after(c, SEG * (h - 1), 1, 0))
                    sp.sem_inc(sp_turn, 1)
                for m, a in enumerate(A_OF):
                    sp.dma_start(a_terms[KL * m:KL * m + KL, :, SEG * h:SEG * h + SEG].rearrange("k u s f -> k u (s f)"),
                                 scr_a[:, a].rearrange("(u k) n -> k u n", k=KL)).then_inc(a_in, 16)
                sp.wait_ge(v_out, half)
                sp.dma_start(vrow[:, h].rearrange("p (u n) s -> p u (n s)", u=U),
                             scr_v.rearrange("(u k) (e n) -> (k e) u n", u=U, e=F8)).then_inc(v_in, 16)

            def tick(c, h, t, par, part=None):
                b = t - 1
                if on(c, b):
                    sp.wait_ge(s_sb, after(c, b, NRND, NRND))
                    sp.sem_inc(sp_turn, 1)
                    for q in range(Q):
                        src = s_st[K * q:K * q + F8].rearrange("e t g n -> e (t g) n")
                        row = b % STEPS + K * q if isinstance(b, int) else b + K * q
                        dst = scr_s[bass.ds(chunk_of(c, b), 1), :, bass.ds(row, 1)]
                        dst = dst.rearrange("o (x e) b g -> e (o x) (b g)", e=F8)
                        sp.dma_start(dst, src).then_inc(s_out, 16)
                b = t + 2
                if on(c, b):
                    sp.wait_ge(b_seq, after(c, b, KB, KB))
                    sp.sem_inc(sp_turn, 1)
                    sp.wait_ge(split_seq, after(c, b, KPL, KPL))
                    sp.dma_start(scr_t[par], t_split[:]).then_inc(t_out, 16)
                    sp.wait_ge(t_out, after(c, b, 16, 16))
                    sp.sem_inc(sp_turn, 1)
                    if not early(c, b, 2):
                        sp.wait_ge(phi_ready, after(c, b, NPAIR, -NPAIR))
                        sp.sem_inc(sp_turn, 1)
                    for m, s in enumerate(T_OF):
                        sp.dma_start(t_rows[par][KL * m:KL * m + KL],
                                     scr_t[par, :, s].rearrange("(u k) g -> k u g", k=KL)).then_inc(t_in[par], 16)
                if part == PEEL - 1:
                    store_prepared(*next_half(c, h))

            store_prepared(0, 0)
            pipeline(sp, tick)
            sp.wait_ge(s_out, CH * STEPS * 16 * Q + 1)

        @block.gpsimd
        def _(pool):
            start_at_one(pool, logit_seq, x_ready, vst_ready, split_seq)

            def gather(c, fields):
                if fields[0] == 0:
                    pool.dma_start(ids_sb[:], ids[bass.ds(c, 1)].rearrange("o p f -> (o p) f")).then_inc(ids_in, 16)
                    pool.wait_ge(ids_in, c * 16 + 16)
                    pool.wait_ge(emb_taken, chunks(c, 1))
                    pool.sem_inc(pool_turn, 1)
                for f in fields:
                    nc.gpsimd.indirect_dma_start(
                        out=emb[:, f * K:f * K + K], out_offset=None, in_=tables[f],
                        in_offset=bass.IndirectOffsetOnAxis(ap=ids_sb[:, f:f + 1], axis=0)).then_inc(emb_in, 16)

            def tick(c, h, t, par, part=None):
                n, l, a = t, t + 2, t + 3
                x = prob[1 - par]
                if on(c, a):
                    if not early(c, a, 2):
                        pool.wait_ge(xt_ps, after(c, a, TG, -TG))
                    if isinstance(a, int):
                        pool.wait_ge(prep_seq, prepared(c, a, KPREP) - (KPREP - KLOGIT))
                    nc.gpsimd.tensor_tensor(x[:],
                                            a0[:, at(a)].rearrange("p o f -> p (o f)").unsqueeze(2).to_broadcast([P, F, F]),
                                            q0[:, at(a)].to_broadcast([P, F, F]),
                                            ALU.mult).then_inc(logit_seq, 1)
                    pool.wait_ge(logit_seq, after(c, a, 2, 1))
                    nc.gpsimd.tensor_tensor(x[:], x[:], m0[:, at(a)].to_broadcast([P, F, F]),
                                            ALU.subtract).then_inc(logit_seq, 1)
                if on(c, n):
                    if not early(c, n, 2):
                        pool.wait_ge(s_ps, after(c, n, NRND, -NRND))
                    if isinstance(n, int):
                        pool.wait_ge(v_in, prepared(c, n, 16))
                    hn, bn = half_of(n, h)
                    nc.gpsimd.tensor_tensor(vst[par][:],
                                            vrow[:, hn, :, bn].to_broadcast([P, U * FG, F8]),
                                            f8sel[:].unsqueeze(1).to_broadcast([P, U * FG, F8]),
                                            ALU.mult).then_inc(vst_ready, 1)
                if part is not None and h == 0:
                    n_f = F // PEEL
                    gather(c + 1, range(n_f * part, n_f * part + n_f))
                if on(c, l):
                    pool.wait_ge(b_seq, after(c, l, KB, 1))
                    pool.wait_ge(t_out, after(c, l, 16, 0))
                    pool.sem_inc(pool_turn, 1)
                    nc.gpsimd.tensor_copy(t_split[:, 0], t_f[:]).then_inc(split_seq, 1)
                    pool.wait_ge(split_seq, after(c, l, KPL, 1))
                    nc.gpsimd.tensor_tensor(t_d[:], t_f[:], t_split[:, 0], ALU.subtract).then_inc(split_seq, 1)
                    pool.wait_ge(split_seq, after(c, l, KPL, 2))
                    pool.sem_inc(pool_turn, 1)
                    nc.gpsimd.tensor_copy(t_split[:, 1], t_d[:]).then_inc(split_seq, 1)
                    pool.wait_ge(split_seq, after(c, l, KPL, 3))
                    nc.gpsimd.tensor_tensor(t_split[:, 2], t_d[:], t_split[:, 1], ALU.subtract).then_inc(split_seq, 1)
                if on(c, a):
                    if isinstance(a, int):
                        pool.wait_ge(prep_seq, prepared(c, a, KPREP))
                    pool.wait_ge(a_seq, after(c, a, KA, KA))
                    nc.gpsimd.tensor_tensor(x[:], x[:],
                                            v0[:, at(a)].rearrange("p o f -> p (o f)").unsqueeze(2).to_broadcast([P, F, F]),
                                            ALU.mult).then_inc(x_ready, 1)

            gather(0, range(F))
            pool.wait_ge(consts_in, 16 * 15)
            pipeline(pool, tick)
            pool.wait_ge(emb_in, (CH + 1) * 16 * F)

        @block.vector
        def _(dve):
            start_at_one(dve, prep_seq, emb_taken, a_seq, b_seq, diag_ready, rz_ready, norm_done)
            dve.memset(a_terms[6 * KL:P].rearrange("p u s f -> p (u s f)"), -1.0).then_inc(cleared, 1)
            for ps in ps_sums:
                dve.memset(ps[:], 0.0).then_inc(cleared, 1)
            dve.memset(ps_o[:], 0.0).then_inc(cleared, 1)
            dve.wait_ge(consts_in, 16 * 15)

            def prepare(c, h, part):
                done = [KPREP // PEEL * part]

                def then(ins):
                    done[0] += 1
                    ins.then_inc(prep_seq, 1)

                def prior():
                    dve.wait_ge(prep_seq, chunks(c, 2 * KPREP, h * KPREP + done[0]))

                def w(name):
                    return wk[:, CW[name]].unsqueeze(1).to_broadcast([P, SEG, F])

                here = slice(SEG * h, SEG * h + SEG)
                a_h, q_h, v_h, m_h = (x[:, here] for x in (a0, q0, v0, m0))
                hi0, lo0, hi1, lo1 = (ext[:, i, here] for i in range(4))
                rows = emb_k[:, :, here]
                by_step = rows.rearrange("p f s -> p s f")

                def over_fields(x):
                    return x.unsqueeze(2).to_broadcast([P, SEG, F])

                if part == 0:
                    if h == 0:
                        dve.wait_ge(emb_in, c * (16 * F) + 16 * F)
                        nc.vector.transpose(emb_k[:].rearrange("p f s -> p (f s)"), emb[:]).then_inc(emb_taken, 1)
                        dve.wait_ge(emb_taken, chunks(c, 1, 1))
                    if not early(c, h, 2):
                        dve.wait_ge(x_ready, after(c, SEG * (h - 1), 1, 0))
                    then(nc.vector.tensor_tensor(a_h, by_step, w("a"), ALU.mult))
                    then(nc.vector.tensor_tensor(q_h, by_step, w("q"), ALU.mult))
                if part == 1:
                    prior()
                    then(nc.vector.tensor_reduce(hi0, a_h, AX.X, ALU.max))
                    then(nc.vector.tensor_reduce(lo0, a_h, AX.X, ALU.min))
                if part == 2:
                    prior()
                    then(nc.vector.tensor_tensor(m_tmp[:], q_h, over_fields(hi0), ALU.mult))
                    then(nc.vector.tensor_tensor(m_h, q_h, over_fields(lo0), ALU.mult))
                if part == 3:
                    prior()
                    then(nc.vector.tensor_tensor(m_h, m_h, m_tmp[:], ALU.max))
                    then(nc.vector.tensor_tensor(v_h, by_step, w("v"), ALU.mult))
                if part == 4:
                    if not early(c, h, 1):
                        dve.wait_ge(a_out, chunks(c, 2 * 16, h * 16))
                        dve.wait_ge(v_out, chunks(c, 2 * 16, h * 16))
                    then(nc.vector.tensor_tensor(a1_f[:], by_step, w("a1"), ALU.mult))
                    then(nc.vector.tensor_tensor(v1_k[:], rows, wk[:, CW["v1"]].unsqueeze(2).to_broadcast([P, F, SEG]),
                                                 ALU.mult))
                if part == 5:
                    prior()
                    then(nc.vector.tensor_reduce(hi1, a1_f[:], AX.X, ALU.max))
                    then(nc.vector.tensor_reduce(lo1, a1_f[:], AX.X, ALU.min))
                if part == 6:
                    prior()
                    then(nc.vector.tensor_copy(split(0), by_group(a1_f[:])))
                    prior()
                    then(nc.vector.tensor_tensor(by_group(a1_f[:]), by_group(a1_f[:]), split(0), ALU.subtract))
                if part == 7:
                    prior()
                    then(nc.vector.tensor_copy(split(1), by_group(a1_f[:])))
                    prior()
                    then(nc.vector.tensor_tensor(split(2), by_group(a1_f[:]), split(1), ALU.subtract))

            def by_group(x):
                return x.rearrange("p s (e g) -> p s g e", e=F8)

            def split(i):
                return a_split[:, i].rearrange("p s (g e) -> p s g e", e=F8)

            def make_diag(c, b, kh):
                if isinstance(b, int):
                    dve.wait_ge(a_in, prepared(c, b, 16 * len(A_OF)))
                if not early(c, b, 1):
                    dve.wait_ge(phi_ready, after(c, b, NPAIR, -NPAIR + NPAIR // KH * (kh + 1)))
                mask = diag[:].unsqueeze(1).to_broadcast([P, FG, KL, F8])
                for q in range(Q):
                    src = a_terms[:, q * KH + kh, at(b)].rearrange("p o (g e) -> p (o g) e", e=F8)
                    last = nc.vector.tensor_tensor(a_diag[:, kh, q].rearrange("p g (k e) -> p g k e", e=F8), mask,
                                                   src.unsqueeze(2).to_broadcast([P, FG, KL, F8]), ALU.mult)
                last.then_inc(diag_ready, 1)

            def tick(c, h, t, par, part=None):
                n, m, a, l, d = t, t - 1, t + 3, t + 2, t + 1
                x = prob[1 - par]

                def normalise(r):
                    if on(c, m):
                        kh, qh = divmod(r, 2)
                        dve.wait_ge(rrep_ready, after(c, m, 4, r + 1))
                        e = ex[1 - par][:, kh * FG:kh * FG + FG, 2 * qh:2 * qh + 2, :].rearrange("p g q n -> p g (q n)")
                        nc.vector.tensor_tensor(e, e, ps_r[r % 2][:, 0:2 * G].unsqueeze(1).to_broadcast([P, FG, 2 * G]),
                                                ALU.mult).then_inc(norm_done, 1)

                if on(c, m):
                    dve.wait_ge(z_ready, after(c, m, 1, 1))
                    dve.wait_ge(rrep_ready, after(c, m, 4, 0))
                    nc.vector.reciprocal(rz[:], ps_z[:, 0:G]).then_inc(rz_ready, 1)
                normalise(0)
                if part is not None:
                    prepare(*next_half(c, h), part)
                normalise(1)
                if on(c, n):
                    make_diag(c, n, 1)
                normalise(2)
                normalise(3)
                if on(c, a):
                    dve.wait_ge(l0_exp, after(c, a, 1, 1))
                    nc.vector.tensor_reduce(zr0[:, 0], x[:].rearrange("p f g -> p g f"), AX.X, ALU.add).then_inc(a_seq, 1)
                if on(c, l):
                    dve.wait_ge(out0_ready, after(c, l, 1, 1))
                    dve.wait_ge(split_seq, after(c, l, KPL, 0))
                    nc.vector.tensor_tensor(t_f[:], out0[:], wq1[:], ALU.mult).then_inc(b_seq, 1)
                if on(c, l):
                    dve.wait_ge(b_seq, after(c, l, KB, 1))
                    nc.vector.tensor_scalar(m_u[:], t_f[:], ext[:, 2, at(l)], None, ALU.mult).then_inc(b_seq, 1)
                if on(c, a):
                    dve.wait_ge(a_seq, after(c, a, KA, 1))
                    nc.vector.reciprocal(zr0[:, 1], zr0[:, 0]).then_inc(a_seq, 1)
                if on(c, l):
                    dve.wait_ge(b_seq, after(c, l, KB, 2))
                    nc.vector.scalar_tensor_tensor(out=m_f[:], in0=t_f[:], scalar=ext[:, 3, at(l)], in1=m_u[:],
                                                   op0=ALU.mult, op1=ALU.max).then_inc(b_seq, 1)
                if on(c, a):
                    dve.wait_ge(a_seq, after(c, a, KA, 2))
                    nc.vector.tensor_tensor(x[:], x[:], zr0[:, 1].unsqueeze(1).to_broadcast([P, F, F]),
                                            ALU.mult).then_inc(a_seq, 1)
                if on(c, l):
                    dve.wait_ge(b_seq, after(c, l, KB, 3))
                    dve.wait_ge(t_out, after(c, l, 16, 0))
                    nc.vector.tensor_copy(t_split[:, 3], m_f[:]).then_inc(b_seq, 1)
                if on(c, d):
                    make_diag(c, d, 0)
                if on(c, l):
                    dve.wait_ge(b_seq, after(c, l, KB, 4))
                    nc.vector.tensor_tensor(t_split[:, 4], m_f[:], t_split[:, 3], ALU.subtract).then_inc(b_seq, 1)

            dve.wait_ge(cleared, 5)
            for part in range(PEEL):
                prepare(0, 0, part)
            pipeline(dve, tick)

        @block.scalar
        def _(act):
            start_at_one(act, l0_exp, xt_sb, out0_ready, z0_sb, ex_ready, s_sb)
            act.wait_ge(cleared, 5)

            def tick(c, h, t, par, part=None):
                n, m, a, l = t, t - 1, t + 3, t + 2

                def sums(rnd):
                    w = min(2, FG - 2 * rnd)
                    act.wait_ge(s_ps, after(c, m, NRND, rnd + 1))
                    if rnd == 0:
                        act.wait_ge(s_out, after(c, m, 16 * Q, 0))
                    nc.scalar.copy(s_st[:].rearrange("p t g n -> p g t n")[:, 2 * rnd:2 * rnd + w],
                                   ps_sums[rnd][:].rearrange("p (g x) -> p g x", g=2)[:, 0:w, 0:GT * GP]
                                   .rearrange("p g (t n) -> p g t n", t=GT)).then_inc(s_sb, 1)

                for j in range(GRP):
                    if on(c, n):
                        for p in (2 * j, 2 * j + 1):
                            if p == 0 and not early(c, n, 2):
                                act.wait_ge(s_ps, after(c, n, NRND, -NRND))
                            act.wait_ge(phi_ready, after(c, n, NPAIR, p + 1))
                            qh = p % 2
                            nc.scalar.activation(
                                ex[par][:, j, 2 * qh:2 * qh + 2, :].rearrange("p q g -> p (q g)"),
                                ps_phi[p % BANKS][:, 0:2 * G], ACT.Exp).then_inc(ex_ready, 1)
                    if on(c, l) and j < TG:
                        act.wait_ge(xt_ps, after(c, l, TG, j + 1))
                        if not (early(c, l, 1) and j < 2):
                            act.wait_ge(main_done, after(c, l, TG, j - 1))
                        cols = P * (len(XGS[j]) - (j == TG - 1))
                        ins = nc.scalar.copy(xt[:, j % 2, 0:cols], ps_x[:, 0:cols])
                        if j == TG - 1:
                            rows = C0 - (CT - 1) * P
                            ins = nc.scalar.copy(xt[0:rows, j % 2, cols:cols + P], ps_x[0:rows, cols:cols + P])
                        ins.then_inc(xt_sb, 1)
                    if on(c, a) and j == 3:
                        act.wait_ge(logit_seq, after(c, a, 2, 2))
                        x = prob[1 - par][:].rearrange("p f g -> p (f g)")
                        nc.scalar.activation(x, x, ACT.Exp).then_inc(l0_exp, 1)
                    if on(c, l) and j == 5:
                        act.wait_ge(main_done, after(c, l, TG, TG))
                        act.wait_ge(z0_ps, after(c, l, 1, 0))
                        act.wait_ge(b_seq, after(c, l, KB, 0))
                        nc.scalar.copy(out0[:], ps_o[:, 0:J]).then_inc(out0_ready, 1)
                    if on(c, l) and j == 8:
                        act.wait_ge(z0_ps, after(c, l, 1, 1))
                        dst = z0_t[:].rearrange("p h (c q s) -> p h c q s", c=CH, q=Q)
                        dst = dst[:, :, bass.ds(chunk_of(c, l), 1), :, at(l)].rearrange("p h o q s -> p h (o q s)")
                        nc.scalar.copy(dst, ps_o[:, 256:256 + 2 * Q].rearrange("p (h q) -> p h q", h=2)).then_inc(z0_sb, 1)
                    if on(c, m) and j == GRP - 1:
                        sums(0)
                if on(c, m):
                    sums(1)
                    sums(2)

            pipeline(act, tick)

        @block.tensor
        def _(pe):
            start_at_one(pe, xt_ps, main_done, z0_ps, phi_ready, z_ready, rrep_ready, s_ps)
            pe.wait_ge(consts_in, 16 * 15)
            pe.wait_ge(cleared, 5)

            def tick(c, h, t, par, part=None):
                n, m, l = t, t - 1, t + 2

                def logits(p):
                    j, qh = divmod(p, 2)
                    kh, fg = divmod(j, FG)
                    if p == 0:
                        half = 16 * TERMS // 2
                        pe.wait_ge(t_in[par], after(c, n, half, 2 * half - half * par))
                    if qh == 0 and fg == 0:
                        pe.wait_ge(diag_ready, after(c, n, 2, kh + 1))
                    last = p - BANKS if p >= BANKS else max(x for x in range(NPAIR) if x % BANKS == p) - NPAIR
                    if last >= 0 or not early(c, n, 1):
                        pe.wait_ge(ex_ready, after(c, n, NPAIR, last + 1))
                    for i in range(2):
                        q = 2 * qh + i
                        mm = nc.tensor.matmul(ps_phi[p % BANKS][:, i * G:i * G + G], a_diag[:, kh, q, fg, :],
                                              t_rows[par][:, q * KH + kh, :], start=True, stop=True)
                    mm.then_inc(phi_ready, 1)

                def sum_f(j):
                    pe.wait_ge(ex_ready, after(c, n, NPAIR, 2 * j + 2))
                    if j == 0:
                        pe.wait_ge(rz_ready, after(c, n, 1, 0))
                    for q in range(Q):
                        mm = nc.tensor.matmul(ps_z[K * q:K * q + K, 0:G], zsel[:, j // FG, :], ex[par][:, j, q, :],
                                              start=(j == 0), stop=(j == GRP - 1))
                    if j == GRP - 1:
                        mm.then_inc(z_ready, 1)

                def spread(r):
                    kh, qh = divmod(r, 2)
                    if r == 0:
                        pe.wait_ge(rz_ready, after(c, m, 1, 1))
                        pe.wait_ge(s_sb, after(c, m, NRND, 0))
                    pe.wait_ge(norm_done, after(c, m, 4, max(r - 1, 0)))
                    for i in range(2):
                        mm = nc.tensor.matmul(ps_r[r % 2][:, i * G:i * G + G], rsel[:, (2 * qh + i) * KH + kh, :], rz[:],
                                              start=True, stop=True)
                    mm.then_inc(rrep_ready, 1)

                def sum_k(fg):
                    if fg == 0:
                        pe.wait_ge(norm_done, after(c, m, 4, 4))
                        pe.wait_ge(vst_ready, after(c, m, 1, 1))
                    for kh in range(KH):
                        for q in range(Q):
                            mm = nc.tensor.matmul(
                                ps_sums[fg // 2][K * q:K * q + F8, 256 * (fg % 2):256 * (fg % 2) + G],
                                vst[1 - par][:, (q * KH + kh) * FG + fg, :], ex[1 - par][:, kh * FG + fg, q, :],
                                start=(kh == 0), stop=(kh == KH - 1))
                    if fg % 2 or fg == FG - 1:
                        mm.then_inc(s_ps, 1)

                def turn(g):
                    if g == 0:
                        pe.wait_ge(x_ready, after(c, l, 1, 1))
                    pe.wait_ge(xt_sb, after(c, l, TG, g))
                    x = prob[par][:].rearrange("p f g -> p (f g)")
                    for i, ct in enumerate(XGS[g]):
                        w = min(P, C0 - ct * P)
                        mm = nc.tensor.transpose(ps_x[0:w, i * P:i * P + P], x[:, ct * P:ct * P + w], ident[:])
                    mm.then_inc(xt_ps, 1)

                def layer1(g, tiles):
                    if 0 in tiles:
                        pe.wait_ge(xt_sb, after(c, l, TG, g + 1))
                    if g == 0:
                        pe.wait_ge(z0_sb, after(c, l, 1, 0))
                    for i in tiles:
                        ct = XGS[g][i]
                        w = min(P, C0 - ct * P)
                        mm = nc.tensor.matmul(ps_o[:, 0:J], xt[0:w, g % 2, i * P:i * P + P], cw0_sb[0:w, ct, :],
                                              start=(ct == 0), stop=(ct == CT - 1))
                    if i == len(XGS[g]) - 1:
                        mm.then_inc(main_done, 1)

                for j in range(GRP):
                    if on(c, n):
                        logits(2 * j)
                        logits(2 * j + 1)
                        if j:
                            sum_f(j - 1)
                    if on(c, l):
                        if j < TG:
                            turn(j)
                        if 1 <= j < TG:
                            layer1(j - 1, range(len(XGS[j - 1])))
                        if j == TG:
                            layer1(TG - 1, range(2))
                        if j == TG + 1:
                            layer1(TG - 1, range(2, len(XGS[TG - 1])))
                    if on(c, m) and j < 4:
                        spread(j)
                    if on(c, l):
                        if j == 7:
                            pe.wait_ge(out0_ready, after(c, l, 1, 1))
                            for h, j0, w in ZC:
                                mm = nc.tensor.matmul(ps_o[0:w, 256 + Q * h:256 + Q * h + Q], out0[:, j0:j0 + w],
                                                      onesq[:], start=True, stop=True)
                            mm.then_inc(z0_ps, 1)
                    if on(c, m) and j > GRP - FG:
                        sum_k(j - (GRP - FG + 1))
                if on(c, n):
                    sum_f(GRP - 1)
                if on(c, m):
                    sum_k(FG - 1)

            pipeline(pe, tick)


def dense_layers(nc, dense_t, cw1, w1, b1, w2, b2, w3, ident_c, scr_s, z0_t, z1_t, y):
    n1, n2 = H1 // P, H2 // P
    z_rows = [(0, z0_t, 0, P), (1, z0_t, 1, J - P), (2, z1_t, 0, P), (3, z1_t, 1, J - P)]
    n_w = 9
    with ExitStack() as ctx:
        def sb(name, shape, dt=F32):
            return ctx.enter_context(nc.sbuf_tensor(name, shape, dt))

        def psum(name):
            return ctx.enter_context(nc.psum_tensor(name, [P, 512], F32))

        def sem(name):
            return ctx.enter_context(nc.semaphore(name))

        cw1_sb = sb("cw1_sb", [R1, GP, J])
        s_rows = [sb(f"s_rows{i}", [R1, P, GP]) for i in range(2)]
        w1_sb = sb("w1_sb", [P, 5, H1])
        w2_sb = sb("w2_sb", [P, n1, H2])
        w3_sb = sb("w3_sb", [P, n2])
        b1_sb = sb("b1_sb", [P, n1])
        b2_sb = sb("b2_sb", [P, n2])
        dense_sb = sb("dense_sb", [DD, B])
        ident = sb("ident2", [P, P])
        z1_b = sb("z1_b", [P, J])
        h1 = sb("h1", [P, n1, B])
        h2 = sb("h2", [P, n2, B])
        y_sb = sb("y_sb", [1, B])
        ps_z1 = psum("ps_z1")
        ps_t = psum("ps_t")
        ps_h = [psum(f"ps_h{i}") for i in range(4)]

        cw1_in = [sem(f"cw1_in{i}") for i in range((GP + PIECE - 1) // PIECE)]
        srow_in = [sem(f"srow_in{i}") for i in range(2)]
        weights_in = sem("weights_in")
        z1_ps = sem("z1_ps")
        z1_sb = sem("z1_sb")
        z1t_ps = sem("z1t_ps")
        z1t_sb = sem("z1t_sb")
        h_ps = sem("h_ps")
        h_sb = sem("h_sb")
        y_out = sem("y_out")

        block = ctx.enter_context(nc.Block())

        @block.sync
        def _(sp):
            sp.dma_start(s_rows[0][:], scr_s[0]).then_inc(srow_in[0], 16)
            for g in range(0, GP, PIECE):
                w = min(PIECE, GP - g)
                sp.dma_start(cw1_sb[:, g:g + w], cw1[:, g:g + w]).then_inc(cw1_in[g // PIECE], 16)
            sp.dma_start(s_rows[1][:], scr_s[1]).then_inc(srow_in[1], 16)
            sp.dma_start(ident[:], ident_c).then_inc(weights_in, 16)
            for i, r0, rows in ((0, 0, P), (1, P, J - P), (2, J, P), (3, J + P, J - P), (4, 2 * J, DD)):
                sp.dma_start(w1_sb[0:rows, i], w1[r0:r0 + rows]).then_inc(weights_in, 16)
            for dst, src in ((w2_sb, w2), (w3_sb, w3), (b1_sb, b1), (b2_sb, b2), (dense_sb, dense_t)):
                sp.dma_start(dst[:], src).then_inc(weights_in, 16)
            for c in range(2, CH):
                sp.wait_ge(z1_ps, c - 1)
                sp.dma_start(s_rows[c % 2][:], scr_s[c]).then_inc(srow_in[c % 2], 16)
            sp.wait_ge(h_sb, n1 + n2 + 1)
            sp.dma_start(y, y_sb[:]).then_inc(y_out, 16)
            sp.wait_ge(y_out, 16)

        @block.tensor
        def _(pe):
            pe.sem_inc(z1t_ps, 1)

            def turn(c):
                pe.wait_ge(z1_sb, c + 2)
                pe.wait_ge(weights_in, 16 * 11)
                pe.wait_ge(z1t_sb, c + 1)
                for h, j0, w in ZC:
                    mm = nc.tensor.transpose(ps_t[0:w, h * P:h * P + P], z1_b[:, j0:j0 + w], ident[:])
                mm.then_inc(z1t_ps, 1)

            with pe.Fori(0, CH // 2) as pair:
                for i in range(2):
                    c = pair * 2 + i
                    pe.wait_ge(srow_in[i], pair * 16 + 16)
                    pe.wait_ge(z1_sb, c + 1)
                    for g in range(GP):
                        if g % PIECE == 0:
                            pe.wait_ge(cw1_in[g // PIECE], 16)
                        mm = nc.tensor.matmul(ps_z1[:, 0:J], s_rows[i][:, :, g], cw1_sb[:, g, :],
                                              start=(g == 0), stop=(g == GP - 1))
                    mm.then_inc(z1_ps, 1)
                    turn(c)
            pe.wait_ge(z1t_sb, CH + 1)
            for m in range(n1):
                for i, z, h, rows in z_rows:
                    nc.tensor.matmul(ps_h[m % 4][:], w1_sb[0:rows, i, m * P:m * P + P], z[0:rows, h, :],
                                     start=(i == 0), stop=False)
                nc.tensor.matmul(ps_h[m % 4][:], w1_sb[0:DD, 4, m * P:m * P + P], dense_sb[:],
                                 start=False, stop=True).then_inc(h_ps, 1)
            pe.wait_ge(h_sb, n1)
            for m in range(n2):
                for i in range(n1):
                    mm = nc.tensor.matmul(ps_h[m][:], w2_sb[:, i, m * P:m * P + P], h1[:, i, :],
                                          start=(i == 0), stop=(i == n1 - 1))
                mm.then_inc(h_ps, 1)
            pe.wait_ge(h_sb, n1 + n2)
            for m in range(n2):
                mm = nc.tensor.matmul(ps_h[2][0:1, :], w3_sb[:, m:m + 1], h2[:, m, :], start=(m == 0), stop=(m == n2 - 1))
            mm.then_inc(h_ps, 1)

        @block.scalar
        def _(act):
            act.sem_inc(z1_sb, 1)
            act.sem_inc(z1t_sb, 1)
            with act.Fori(0, CH) as c:
                act.wait_ge(z1_ps, c + 1)
                act.wait_ge(z1t_ps, c + 1)
                nc.scalar.copy(z1_b[:], ps_z1[:, 0:J]).then_inc(z1_sb, 1)
                act.wait_ge(z1t_ps, c + 2)
                for h, j0, w in ZC:
                    ins = nc.scalar.copy(z1_t[0:w, h, bass.ds(c * P, P)], ps_t[0:w, h * P:h * P + P])
                ins.then_inc(z1t_sb, 1)
            act.wait_ge(weights_in, 16 * 11)
            for m in range(n1):
                act.wait_ge(h_ps, m + 1)
                nc.scalar.activation(h1[:, m, :], ps_h[m % 4][:], ACT.Relu, bias=b1_sb[:, m:m + 1]).then_inc(h_sb, 1)
            for m in range(n2):
                act.wait_ge(h_ps, n1 + m + 1)
                nc.scalar.activation(h2[:, m, :], ps_h[m][:], ACT.Relu, bias=b2_sb[:, m:m + 1]).then_inc(h_sb, 1)
            act.wait_ge(h_ps, n1 + n2 + 1)
            nc.scalar.copy(y_sb[:], ps_h[2][0:1, :]).then_inc(h_sb, 1)


def kernel(**inputs):
    import ml_dtypes
    import numpy as np
    import concourse.bacc as bacc
    from concourse.bass_utils import run_bass_kernel_spmd

    x = {k: np.asarray(v) for k, v in inputs.items()}
    p = np.arange(P)
    zsel = np.zeros((P, KH, K), np.float32)
    rsel = np.zeros((P, U, P), np.float32)
    for kh in range(KH):
        zsel[p, kh, kh * KL + p // F8] = 1
    for u in range(U):
        rsel[u * KL + p // F8, u, p] = 1
    diag = (p[:, None, None] % KL == np.arange(KL)[None, :, None]) * np.ones((1, 1, F8))
    f8sel = (p[:, None] % F8 == np.arange(F8)[None]) * 1.0
    onesq = (p[:, None] // K == np.arange(Q)[None]) * 1.0

    def rows(name):
        return x["L0_rec_" + name][0].T

    cw0 = np.pad(x["L0_rec_cw0"][0], ((0, CT * P - C0), (0, 0))).reshape(CT, P, J).transpose(1, 0, 2)
    cw1 = np.pad(x["L0_rec_cw1"][0].reshape(F8, FG, G, J), ((0, 0), (0, 0), (0, GT * GP - G), (0, 0)))
    cw1 = cw1.reshape(F8, FG, GT, GP, J).transpose(2, 1, 0, 3, 4).reshape(R1, GP, J)
    arrays = {
        "dense_t": x["dense_ctx"].T, "ids": np.concatenate([x["ids"], x["ids"][:P]]).reshape(CH + 1, P, F),
        "w_k": np.stack([rows("wk0"), rows("wq0"), rows("wv0"), rows("wk1"), rows("wv1")], 1), "wq1_t": rows("wq1"),
        "cw0": cw0, "cw1": cw1, "w1": x["W_top1"], "b1": x["b_top1"].reshape(-1, P).T,
        "w2": x["W_top2"].reshape(-1, P, H2).transpose(1, 0, 2), "b2": x["b_top2"].reshape(-1, P).T,
        "w3": x["W_top3"].reshape(-1, P).T, "ident": np.eye(P, dtype=np.float32), "zsel": zsel, "rsel": rsel,
        "diag": diag.astype(ml_dtypes.bfloat16), "f8sel": f8sel.astype(np.float32), "onesq": onesq.astype(np.float32),
    }
    arrays.update({f"tbl_{f}": x[f"tbl_{f}"] for f in range(F)})
    arrays = {k: np.ascontiguousarray(v) for k, v in arrays.items()}
    nc = bacc.Bacc("TRN2", target_bir_lowering=False, num_devices=1)
    d = {k: nc.dram_tensor("in_" + k, v.shape, mybir.dt.from_np(v.dtype), kind="ExternalInput").ap() for k, v in arrays.items()}
    y = nc.dram_tensor("y", (1, B), F32, kind="ExternalOutput").ap()
    dlrm_cin_tower(nc, d["dense_t"], d["ids"], [d[f"tbl_{f}"] for f in range(F)], d["w_k"], d["wq1_t"], d["cw0"],
                   d["cw1"], d["w1"], d["b1"], d["w2"], d["b2"], d["w3"], d["ident"], d["zsel"], d["rsel"],
                   d["diag"], d["f8sel"], d["onesq"], y)
    r = run_bass_kernel_spmd(nc, [{"in_" + k: v for k, v in arrays.items()}], core_ids=[0])
    return r.results[0]["y"].reshape(B, 1)
```

```python
from contextlib import ExitStack

import concourse.bass as bass
from concourse import mybir

F32 = mybir.dt.float32
BF16 = mybir.dt.bfloat16
I32 = mybir.dt.int32
ALU = mybir.AluOpType
ACT = mybir.ActivationFunctionType
AX = mybir.AxisListType

P = 128
B = 512
F = 40
K = 32
J = 200
G = J
CH = B // P
Q = 4
STEPS = P // Q
KH = 2
KL = K // KH
F8 = 8
FG = F // F8
U = Q * KH
NPAIR = KH * FG * Q // 2
GRP = KH * FG
C0 = F * F
CT = (C0 + P - 1) // P
XG = 4
XGS = [range(0, 4), range(4, 7), range(7, 10), range(10, CT)]
TG = len(XGS)
GT = 3
GP = (G + GT - 1) // GT
R1 = GT * F
TERMS = 8
A_OF = [0, 1, 2, 0, 1, 0]
T_OF = [0, 0, 0, 1, 1, 2, 3, 4]
NT = 5
H1 = 512
H2 = 256
DD = 16
ZC = [(0, 0, P), (1, P, J - P)]
BANKS = 2
CW = {"a": 0, "q": 1, "v": 2, "a1": 3, "v1": 4}
KA = 3
KB = 3
KD = 2
KR = 5
PARTS = 3
ROUNDS = [range(0, 2), range(2, 3), range(3, FG)]
NRND = len(ROUNDS)
KPREP = 16
SEG = STEPS // 2
PEEL = 8
KLOGIT = 7
KPL = 6
PIECE = 17
REUSED = [5 * STEPS * F + 2 * F * F, CT * J + 5 * G, U * STEPS * F // 2]


def dlrm_cin_tower(nc, dense_t, ids, tables, w_k, wq1_t, cw0, cw1, w1, b1, w2, b2, w3,
                   ident_c, zsel_c, rsel_c, diag_c, f8sel_c, onesq_c, y):
    scr_t = nc.dram_tensor("scr_t", (2, P, NT, G), BF16, kind="Internal").ap()
    scr_a = nc.dram_tensor("scr_a", (P, 3, SEG * F), BF16, kind="Internal").ap()
    scr_v = nc.dram_tensor("scr_v", (P, F * SEG), F32, kind="Internal").ap()
    scr_s = nc.dram_tensor("scr_s", (CH, R1, P, GP), F32, kind="Internal").ap()

    with ExitStack() as ctx:
        z0_t = ctx.enter_context(nc.sbuf_tensor("z0_t", [P, 2, B], F32))
        z1_t = ctx.enter_context(nc.sbuf_tensor("z1_t", [P, 2, B], F32))
        ident = ctx.enter_context(nc.sbuf_tensor("ident", [P, P], F32))
        s_st = ctx.enter_context(nc.sbuf_tensor("s_st", [P, GT, FG, GP], F32))
        s_out = ctx.enter_context(nc.semaphore("s_out"))
        reused = [ctx.enter_context(nc.sbuf_tensor(f"reused{i}", [P, n], F32)) for i, n in enumerate(REUSED)]
        first_in = [ctx.enter_context(nc.semaphore(f"first_in{i}")) for i in range(3)]
        cin_pipeline(nc, ids, tables, w_k, wq1_t, cw0, cw1, ident_c, zsel_c, rsel_c, diag_c, f8sel_c, onesq_c,
                     scr_t, scr_a, scr_v, scr_s, z0_t, ident, s_st, s_out, reused, first_in)
        dense_layers(nc, dense_t, cw1, w1, b1, w2, b2, w3, scr_s, s_out, z0_t, z1_t, ident, reused, first_in, y)


def first_operands(reused):
    s_rows = reused[0][0:R1, 0:P * GP].rearrange("p (b g) -> p b g", b=P)
    return [s_rows] + [r[0:R1, 0:PIECE * J].rearrange("p (g j) -> p g j", g=PIECE) for r in reused[1:]]


def cin_pipeline(nc, ids, tables, w_k, wq1_t, cw0, cw1, ident_c, zsel_c, rsel_c, diag_c, f8sel_c, onesq_c,
                 scr_t, scr_a, scr_v, scr_s, z0_t, ident, s_st, s_out, reused, first_in):
    with ExitStack() as ctx:
        def sb(name, shape, dt=F32):
            return ctx.enter_context(nc.sbuf_tensor(name, shape, dt))

        def psum(name):
            return ctx.enter_context(nc.psum_tensor(name, [P, 512], F32))

        def sem(name):
            return ctx.enter_context(nc.semaphore(name))

        rest = STEPS * F
        a0, q0, v0, m0 = (reused[0][:, i * rest:(i + 1) * rest].rearrange("p (s f) -> p s f", s=STEPS)
                          for i in range(4))
        emb_k = reused[0][:, 4 * rest:5 * rest].rearrange("p (f s) -> p f s", f=F)
        prob = [reused[0][:, 5 * rest + i * F * F:5 * rest + (i + 1) * F * F].rearrange("p (f g) -> p f g", f=F)
                for i in range(2)]
        cw0_sb = reused[1][:, 0:CT * J].rearrange("p (c j) -> p c j", c=CT)
        out0, t_f, t_d, m_u, m_f = (reused[1][:, CT * J + i * G:CT * J + (i + 1) * G] for i in range(5))
        a_terms = reused[2][:].bitcast(BF16).rearrange("p (u s f) -> p u s f", u=U, s=STEPS)

        zsel = sb("zsel", [P, KH, K])
        rsel = sb("rsel", [P, U, P], BF16)
        diag = sb("diag", [P, KL, F8], BF16)
        f8sel = sb("f8sel", [P, F8])
        onesq = sb("onesq", [P, Q])
        wk = sb("wk", [P, 5, F])
        wq1 = sb("wq1", [P, G])
        ids_sb = sb("ids_sb", [P, F], I32)
        emb = sb("emb", [P, F * K])
        ext = sb("ext", [P, 4, STEPS])
        vrow = sb("vrow", [P, 2, U * FG, SEG])
        a1_f = sb("a1_f", [P, SEG, F])
        m_tmp = sb("m_tmp", [P, SEG, F])
        v1_k = sb("v1_k", [P, F, SEG])
        a_split = sb("a_split", [P, 3, SEG, F], BF16)
        zr0 = sb("zr0", [P, 2, F])
        xt = sb("xt", [P, 2, XG * P])
        t_split = sb("t_split", [P, NT, G], BF16)
        t_rows = [sb(f"t_rows{i}", [P, U, G], BF16) for i in range(2)]
        a_diag = sb("a_diag", [P, KH, Q, FG, KL * F8], BF16)
        ex = [sb(f"ex{i}", [P, GRP, Q, G]) for i in range(2)]
        rz = sb("rz", [P, G])
        rz_split = sb("rz_split", [P, PARTS, G], BF16)
        vst = [sb(f"vst{i}", [P, U * FG, F8]) for i in range(2)]
        ps_phi = [psum(f"ps_phi{i}") for i in range(BANKS)]
        ps_z = psum("ps_z")
        ps_r = [psum(f"ps_r{i}") for i in range(2)]
        ps_s = psum("ps_s")
        ps_sums = [ps_r[0], ps_r[1], ps_s]
        ps_x = psum("ps_x")
        ps_o = psum("ps_o")

        consts_in = sem("consts_in")
        cleared = sem("cleared")
        ids_in = sem("ids_in")
        emb_in = sem("emb_in")
        prep_seq = sem("prep_seq")
        a_out = sem("a_out")
        a_in = sem("a_in")
        v_out = sem("v_out")
        v_in = sem("v_in")
        emb_taken = sem("emb_taken")
        logit_seq = sem("logit_seq")
        x_ready = sem("x_ready")
        a_seq = sem("a_seq")
        l0_exp = sem("l0_exp")
        xt_ps = sem("xt_ps")
        xt_sb = sem("xt_sb")
        main_done = sem("main_done")
        out0_ready = sem("out0_ready")
        z0_ps = sem("z0_ps")
        z0_sb = sem("z0_sb")
        b_seq = sem("b_seq")
        split_seq = sem("split_seq")
        t_out = sem("t_out")
        t_in = [sem(f"t_in{i}") for i in range(2)]
        diag_ready = sem("diag_ready")
        phi_ready = sem("phi_ready")
        ex_ready = sem("ex_ready")
        z_ready = sem("z_ready")
        rz_ready = sem("rz_ready")
        rrep_ready = sem("rrep_ready")
        norm_done = sem("norm_done")
        vst_ready = sem("vst_ready")
        s_ps = sem("s_ps")
        s_sb = sem("s_sb")
        pool_turn = sem("pool_turn")
        sp_turn = sem("sp_turn")

        block = ctx.enter_context(nc.Block())

        def pipeline(eng, tick, at_end=None):
            def segment(c, h):
                for s in range(PEEL):
                    tick(c, h, SEG * h + s - 3, (s + 1) % 2, s)
                with eng.Fori(0, (SEG - PEEL) // 2) as it:
                    tick(c, h, it * 2 + (SEG * h + PEEL - 3), 1)
                    tick(c, h, it * 2 + (SEG * h + PEEL - 2), 0)

            segment(0, 0)
            segment(0, 1)
            with eng.Fori(1, CH) as c:
                segment(c, 0)
                segment(c, 1)
            for t in range(STEPS - 3, STEPS + 2):
                if at_end:
                    at_end(t)
                tick(CH - 1, 1, t, t % 2)

        def on(c, b):
            return not (isinstance(c, int) and isinstance(b, int)) or 0 <= c * STEPS + b < B // Q

        def early(c, b, n):
            return isinstance(c, int) and isinstance(b, int) and c * STEPS + b < n

        def after(c, b, per, more):
            return chunks(c, STEPS * per, b * per + more)

        def chunks(c, per, more=0):
            return c * per + (more + 1)

        def start_at_one(eng, *sems):
            for s in sems:
                eng.sem_inc(s, 1)

        def at(b):
            return bass.ds(b % STEPS if isinstance(b, int) else b, 1)

        def chunk_of(c, b):
            return c - 1 if isinstance(b, int) and b < 0 else c

        def prepared(c, b, per):
            return chunks(c, 2 * per, (b // SEG + 1) * per)

        def next_half(c, h):
            return (c, 1) if h == 0 else (c + 1, 0)

        def half_of(b, h):
            if isinstance(b, int):
                return b % STEPS // SEG, bass.ds(b % SEG, 1)
            return h, bass.ds(b - SEG * h, 1)

        @block.sync
        def _(sp):
            start_at_one(sp, a_out, v_out, a_in, v_in, t_out, t_in[0], t_in[1], s_out)
            for q in range(Q):
                sp.dma_start(wk[K * q:K * q + K], w_k).then_inc(consts_in, 16)
                sp.dma_start(wq1[K * q:K * q + K], wq1_t).then_inc(consts_in, 16)
            for dst, src in ((ident, ident_c), (zsel, zsel_c), (rsel, rsel_c), (diag, diag_c), (f8sel, f8sel_c),
                             (onesq, onesq_c), (cw0_sb, cw0)):
                sp.dma_start(dst[:], src).then_inc(consts_in, 16)

            def store_prepared(c, h):
                half = chunks(c, 2 * 16, (h + 1) * 16)
                sp.wait_ge(prep_seq, chunks(c, 2 * KPREP, (h + 1) * KPREP))
                sp.dma_start(scr_a, a_split[:].rearrange("p t s f -> p t (s f)")).then_inc(a_out, 16)
                sp.dma_start(scr_v, v1_k[:].rearrange("p f s -> p (f s)")).then_inc(v_out, 16)
                sp.wait_ge(a_out, half)
                sp.sem_inc(sp_turn, 1)
                if not early(c, h, 2):
                    sp.wait_ge(diag_ready, after(c, SEG * (h - 1), KD, 0))
                    sp.sem_inc(sp_turn, 1)
                    sp.wait_ge(vst_ready, after(c, SEG * (h - 1), 1, 0))
                    sp.sem_inc(sp_turn, 1)
                for m, a in enumerate(A_OF):
                    sp.dma_start(a_terms[KL * m:KL * m + KL, :, SEG * h:SEG * h + SEG].rearrange("k u s f -> k u (s f)"),
                                 scr_a[:, a].rearrange("(u k) n -> k u n", k=KL)).then_inc(a_in, 16)
                sp.wait_ge(v_out, half)
                sp.dma_start(vrow[:, h].rearrange("p (u n) s -> p u (n s)", u=U),
                             scr_v.rearrange("(u k) (e n) -> (k e) u n", u=U, e=F8)).then_inc(v_in, 16)

            def tick(c, h, t, par, part=None):
                b = t - 2
                if on(c, b):
                    sp.wait_ge(s_sb, after(c, b, NRND, NRND))
                    sp.sem_inc(sp_turn, 1)
                    for q in range(Q):
                        src = s_st[K * q:K * q + F8].rearrange("e t g n -> e (t g) n")
                        row = b % STEPS + K * q if isinstance(b, int) else b + K * q
                        dst = scr_s[bass.ds(chunk_of(c, b), 1), :, bass.ds(row, 1)]
                        dst = dst.rearrange("o (x e) b g -> e (o x) (b g)", e=F8)
                        sp.dma_start(dst, src).then_inc(s_out, 16)
                b = t + 1
                if on(c, b):
                    sp.wait_ge(split_seq, after(c, b, KPL, KPL))
                    sp.dma_start(scr_t[1 - par], t_split[:]).then_inc(t_out, 16)
                    sp.wait_ge(t_out, after(c, b, 16, 16))
                    sp.sem_inc(sp_turn, 1)
                    if not early(c, b, 2):
                        sp.wait_ge(phi_ready, after(c, b, NPAIR, -NPAIR))
                        sp.sem_inc(sp_turn, 1)
                    for m, s in enumerate(T_OF):
                        sp.dma_start(t_rows[1 - par][KL * m:KL * m + KL],
                                     scr_t[1 - par, :, s].rearrange("(u k) g -> k u g", k=KL)).then_inc(t_in[1 - par], 16)
                if part == PEEL - 1:
                    store_prepared(*next_half(c, h))

            def first_loads(t):
                s_rows, *pieces = first_operands(reused)
                if t == STEPS - 1:
                    sp.wait_ge(xt_ps, B // Q * TG + 1)
                    sp.wait_ge(prep_seq, 2 * CH * KPREP + 1 + KPREP)
                    sp.dma_start(s_rows, scr_s[0]).then_inc(first_in[0], 16)
                    sp.wait_ge(main_done, B // Q * TG + 1)
                    sp.wait_ge(split_seq, B // Q * KPL + 1)
                    sp.wait_ge(z0_ps, B // Q + 1)
                    sp.dma_start(pieces[0], cw1[:, 0:PIECE]).then_inc(first_in[1], 16)
                if t == STEPS:
                    sp.wait_ge(diag_ready, B // Q * KD + 1)
                    sp.wait_ge(a_in, 16 * len(A_OF) * (2 * CH + 1) + 1)
                    sp.dma_start(pieces[1], cw1[:, PIECE:2 * PIECE]).then_inc(first_in[2], 16)

            store_prepared(0, 0)
            pipeline(sp, tick, first_loads)

        @block.gpsimd
        def _(pool):
            start_at_one(pool, logit_seq, x_ready, vst_ready, split_seq)

            def gather(c, fields):
                if fields[0] == 0:
                    pool.dma_start(ids_sb[:], ids[bass.ds(c, 1)].rearrange("o p f -> (o p) f")).then_inc(ids_in, 16)
                    pool.wait_ge(ids_in, c * 16 + 16)
                    pool.wait_ge(emb_taken, chunks(c, 1))
                    pool.sem_inc(pool_turn, 1)
                for f in fields:
                    nc.gpsimd.indirect_dma_start(
                        out=emb[:, f * K:f * K + K], out_offset=None, in_=tables[f],
                        in_offset=bass.IndirectOffsetOnAxis(ap=ids_sb[:, f:f + 1], axis=0)).then_inc(emb_in, 16)

            def tick(c, h, t, par, part=None):
                n, d, a = t, t + 1, t + 3
                x = prob[1 - par]
                if on(c, a):
                    if not early(c, a, 2):
                        pool.wait_ge(xt_ps, after(c, a, TG, -TG))
                    if isinstance(a, int):
                        pool.wait_ge(prep_seq, prepared(c, a, KPREP) - (KPREP - KLOGIT))
                    nc.gpsimd.tensor_tensor(x[:],
                                            a0[:, at(a)].rearrange("p o f -> p (o f)").unsqueeze(2).to_broadcast([P, F, F]),
                                            q0[:, at(a)].to_broadcast([P, F, F]),
                                            ALU.mult).then_inc(logit_seq, 1)
                    pool.wait_ge(logit_seq, after(c, a, 2, 1))
                    nc.gpsimd.tensor_tensor(x[:], x[:], m0[:, at(a)].to_broadcast([P, F, F]),
                                            ALU.subtract).then_inc(logit_seq, 1)
                if on(c, n):
                    if not early(c, n, 2):
                        pool.wait_ge(s_ps, after(c, n, NRND, -NRND))
                    if isinstance(n, int):
                        pool.wait_ge(v_in, prepared(c, n, 16))
                    hn, bn = half_of(n, h)
                    nc.gpsimd.tensor_tensor(vst[par][:],
                                            vrow[:, hn, :, bn].to_broadcast([P, U * FG, F8]),
                                            f8sel[:].unsqueeze(1).to_broadcast([P, U * FG, F8]),
                                            ALU.mult).then_inc(vst_ready, 1)
                if on(c, d):
                    pool.wait_ge(b_seq, after(c, d, KB, 1))
                    pool.wait_ge(t_out, after(c, d, 16, 0))
                    pool.sem_inc(pool_turn, 1)
                    nc.gpsimd.tensor_copy(t_split[:, 0], t_f[:]).then_inc(split_seq, 1)
                    pool.wait_ge(split_seq, after(c, d, KPL, 1))
                    nc.gpsimd.tensor_tensor(t_d[:], t_f[:], t_split[:, 0], ALU.subtract).then_inc(split_seq, 1)
                    pool.wait_ge(split_seq, after(c, d, KPL, 2))
                    pool.sem_inc(pool_turn, 1)
                    nc.gpsimd.tensor_copy(t_split[:, 1], t_d[:]).then_inc(split_seq, 1)
                    pool.wait_ge(split_seq, after(c, d, KPL, 3))
                    nc.gpsimd.tensor_tensor(t_split[:, 2], t_d[:], t_split[:, 1], ALU.subtract).then_inc(split_seq, 1)
                    pool.wait_ge(b_seq, after(c, d, KB, KB))
                    pool.sem_inc(pool_turn, 1)
                    nc.gpsimd.tensor_copy(t_split[:, 3], m_f[:]).then_inc(split_seq, 1)
                    pool.wait_ge(split_seq, after(c, d, KPL, 5))
                    nc.gpsimd.tensor_tensor(t_split[:, 4], m_f[:], t_split[:, 3], ALU.subtract).then_inc(split_seq, 1)
                if part is not None and h == 0:
                    n_f = F // PEEL
                    gather(c + 1, range(n_f * part, n_f * part + n_f))
                if on(c, a):
                    if isinstance(a, int):
                        pool.wait_ge(prep_seq, prepared(c, a, KPREP))
                    pool.wait_ge(a_seq, after(c, a, KA, KA))
                    nc.gpsimd.tensor_tensor(x[:], x[:],
                                            v0[:, at(a)].rearrange("p o f -> p (o f)").unsqueeze(2).to_broadcast([P, F, F]),
                                            ALU.mult).then_inc(x_ready, 1)

            gather(0, range(F))
            pool.wait_ge(consts_in, 16 * 15)
            pipeline(pool, tick)
            pool.wait_ge(emb_in, (CH + 1) * 16 * F)

        @block.vector
        def _(dve):
            start_at_one(dve, prep_seq, emb_taken, a_seq, b_seq, diag_ready, rz_ready, norm_done)
            dve.memset(a_terms[6 * KL:P].rearrange("p u s f -> p (u s f)"), -1.0).then_inc(cleared, 1)
            for ps in ps_sums:
                dve.memset(ps[:], 0.0).then_inc(cleared, 1)
            dve.memset(ps_o[:], 0.0).then_inc(cleared, 1)
            dve.wait_ge(consts_in, 16 * 15)

            def prepare(c, h, part):
                done = [KPREP // PEEL * part]

                def then(ins):
                    done[0] += 1
                    ins.then_inc(prep_seq, 1)

                def prior():
                    dve.wait_ge(prep_seq, chunks(c, 2 * KPREP, h * KPREP + done[0]))

                def w(name):
                    return wk[:, CW[name]].unsqueeze(1).to_broadcast([P, SEG, F])

                here = slice(SEG * h, SEG * h + SEG)
                a_h, q_h, v_h, m_h = (x[:, here] for x in (a0, q0, v0, m0))
                hi0, lo0, hi1, lo1 = (ext[:, i, here] for i in range(4))
                rows = emb_k[:, :, here]
                by_step = rows.rearrange("p f s -> p s f")

                def over_fields(x):
                    return x.unsqueeze(2).to_broadcast([P, SEG, F])

                if part == 0:
                    if h == 0:
                        dve.wait_ge(emb_in, c * (16 * F) + 16 * F)
                        nc.vector.transpose(emb_k[:].rearrange("p f s -> p (f s)"), emb[:]).then_inc(emb_taken, 1)
                        dve.wait_ge(emb_taken, chunks(c, 1, 1))
                    if not early(c, h, 2):
                        dve.wait_ge(x_ready, after(c, SEG * (h - 1), 1, 0))
                    then(nc.vector.tensor_tensor(a_h, by_step, w("a"), ALU.mult))
                    then(nc.vector.tensor_tensor(q_h, by_step, w("q"), ALU.mult))
                if part == 1:
                    prior()
                    then(nc.vector.tensor_reduce(hi0, a_h, AX.X, ALU.max))
                    then(nc.vector.tensor_reduce(lo0, a_h, AX.X, ALU.min))
                if part == 2:
                    prior()
                    then(nc.vector.tensor_tensor(m_tmp[:], q_h, over_fields(hi0), ALU.mult))
                    then(nc.vector.tensor_tensor(m_h, q_h, over_fields(lo0), ALU.mult))
                if part == 3:
                    prior()
                    then(nc.vector.tensor_tensor(m_h, m_h, m_tmp[:], ALU.max))
                    then(nc.vector.tensor_tensor(v_h, by_step, w("v"), ALU.mult))
                if part == 4:
                    if not early(c, h, 1):
                        dve.wait_ge(a_out, chunks(c, 2 * 16, h * 16))
                        dve.wait_ge(v_out, chunks(c, 2 * 16, h * 16))
                    then(nc.vector.tensor_tensor(a1_f[:], by_step, w("a1"), ALU.mult))
                    then(nc.vector.tensor_tensor(v1_k[:], rows, wk[:, CW["v1"]].unsqueeze(2).to_broadcast([P, F, SEG]),
                                                 ALU.mult))
                if part == 5:
                    prior()
                    then(nc.vector.tensor_reduce(hi1, a1_f[:], AX.X, ALU.max))
                    then(nc.vector.tensor_reduce(lo1, a1_f[:], AX.X, ALU.min))
                if part == 6:
                    prior()
                    then(nc.vector.tensor_copy(split(0), by_group(a1_f[:])))
                    prior()
                    then(nc.vector.tensor_tensor(by_group(a1_f[:]), by_group(a1_f[:]), split(0), ALU.subtract))
                if part == 7:
                    prior()
                    then(nc.vector.tensor_copy(split(1), by_group(a1_f[:])))
                    prior()
                    then(nc.vector.tensor_tensor(split(2), by_group(a1_f[:]), split(1), ALU.subtract))

            def by_group(x):
                return x.rearrange("p s (e g) -> p s g e", e=F8)

            def split(i):
                return a_split[:, i].rearrange("p s (g e) -> p s g e", e=F8)

            def make_diag(c, b, kh, q0=0, q1=Q):
                if q0 == 0:
                    if isinstance(b, int):
                        dve.wait_ge(a_in, prepared(c, b, 16 * len(A_OF)))
                    if not early(c, b, 1):
                        dve.wait_ge(phi_ready, after(c, b, NPAIR, -NPAIR + NPAIR // KH * (kh + 1)))
                mask = diag[:].unsqueeze(1).to_broadcast([P, FG, KL, F8])
                for q in range(q0, q1):
                    src = a_terms[:, q * KH + kh, at(b)].rearrange("p o (g e) -> p (o g) e", e=F8)
                    ins = nc.vector.tensor_tensor(a_diag[:, kh, q].rearrange("p g (k e) -> p g k e", e=F8), mask,
                                                  src.unsqueeze(2).to_broadcast([P, FG, KL, F8]), ALU.mult)
                if q1 == Q:
                    ins.then_inc(diag_ready, 1)

            def tick(c, h, t, par, part=None):
                n, m, a, l, d = t, t - 1, t + 3, t + 2, t + 1
                x = prob[1 - par]

                def diagonals(q0, q1):
                    if on(c, d):
                        make_diag(c, d, 0, q0, q1)

                def normalise(r):
                    if on(c, m):
                        kh, qh = divmod(r, 2)
                        dve.wait_ge(rrep_ready, after(c, m, 4, r + 1))
                        e = ex[1 - par][:, kh * FG:kh * FG + FG, 2 * qh:2 * qh + 2, :].rearrange("p g q n -> p g (q n)")
                        nc.vector.tensor_tensor(e, e, ps_r[r % 2][:, 0:2 * G].unsqueeze(1).to_broadcast([P, FG, 2 * G]),
                                                ALU.mult).then_inc(norm_done, 1)

                if on(c, m):
                    dve.wait_ge(z_ready, after(c, m, 1, 1))
                    dve.wait_ge(rrep_ready, after(c, m, 4, 0))
                    nc.vector.reciprocal(rz[:], ps_z[:, 0:G]).then_inc(rz_ready, 1)
                    dve.wait_ge(rz_ready, after(c, m, KR, 1))
                    nc.vector.tensor_copy(rz_split[:, 0], rz[:]).then_inc(rz_ready, 1)
                    dve.wait_ge(rz_ready, after(c, m, KR, 2))
                    nc.vector.tensor_tensor(rz[:], rz[:], rz_split[:, 0], ALU.subtract).then_inc(rz_ready, 1)
                    dve.wait_ge(rz_ready, after(c, m, KR, 3))
                    nc.vector.tensor_copy(rz_split[:, 1], rz[:]).then_inc(rz_ready, 1)
                    dve.wait_ge(rz_ready, after(c, m, KR, 4))
                    nc.vector.tensor_tensor(rz_split[:, 2], rz[:], rz_split[:, 1], ALU.subtract).then_inc(rz_ready, 1)
                if on(c, n):
                    make_diag(c, n, 1)
                for r in range(4):
                    normalise(r)
                if on(c, a):
                    dve.wait_ge(l0_exp, after(c, a, 1, 1))
                    nc.vector.tensor_reduce(zr0[:, 0], x[:].rearrange("p f g -> p g f"), AX.X, ALU.add).then_inc(a_seq, 1)
                diagonals(0, 1)
                if on(c, a):
                    dve.wait_ge(a_seq, after(c, a, KA, 1))
                    nc.vector.reciprocal(zr0[:, 1], zr0[:, 0]).then_inc(a_seq, 1)
                diagonals(1, 2)
                if on(c, a):
                    dve.wait_ge(a_seq, after(c, a, KA, 2))
                    nc.vector.tensor_tensor(x[:], x[:], zr0[:, 1].unsqueeze(1).to_broadcast([P, F, F]),
                                            ALU.mult).then_inc(a_seq, 1)
                if on(c, l):
                    dve.wait_ge(out0_ready, after(c, l, 1, 1))
                    dve.wait_ge(split_seq, after(c, l, KPL, 0))
                    nc.vector.tensor_tensor(t_f[:], out0[:], wq1[:], ALU.mult).then_inc(b_seq, 1)
                diagonals(2, 3)
                if on(c, l):
                    dve.wait_ge(b_seq, after(c, l, KB, 1))
                    nc.vector.tensor_scalar(m_u[:], t_f[:], ext[:, 2, at(l)], None, ALU.mult).then_inc(b_seq, 1)
                diagonals(3, Q)
                if on(c, l):
                    dve.wait_ge(b_seq, after(c, l, KB, 2))
                    nc.vector.scalar_tensor_tensor(out=m_f[:], in0=t_f[:], scalar=ext[:, 3, at(l)], in1=m_u[:],
                                                   op0=ALU.mult, op1=ALU.max).then_inc(b_seq, 1)
                if part is not None:
                    prepare(*next_half(c, h), part)

            dve.wait_ge(cleared, 5)
            for part in range(PEEL):
                prepare(0, 0, part)
            pipeline(dve, tick)

        @block.scalar
        def _(act):
            start_at_one(act, l0_exp, xt_sb, out0_ready, z0_sb, ex_ready, s_sb)
            act.wait_ge(cleared, 5)

            def tick(c, h, t, par, part=None):
                n, m, k, a, l = t, t - 1, t - 2, t + 3, t + 2

                def sums(m, rnd):
                    w = len(ROUNDS[rnd])
                    fg = ROUNDS[rnd][0]
                    act.wait_ge(s_ps, after(c, m, NRND, rnd + 1))
                    if rnd == 0:
                        act.wait_ge(s_out, after(c, m, 16 * Q, 0))
                    nc.scalar.copy(s_st[:].rearrange("p t g n -> p g t n")[:, fg:fg + w],
                                   ps_sums[rnd][:].rearrange("p (g x) -> p g x", g=2)[:, 0:w, 0:GT * GP]
                                   .rearrange("p g (t n) -> p g t n", t=GT)).then_inc(s_sb, 1)

                for j in range(GRP):
                    if on(c, n):
                        for p in (2 * j, 2 * j + 1):
                            if p == 0 and not early(c, n, 2):
                                act.wait_ge(s_ps, after(c, n, NRND, -NRND - 1))
                            if p == 2 * ROUNDS[2][0] and not early(c, n, 2):
                                act.wait_ge(s_ps, after(c, n, NRND, -NRND))
                            act.wait_ge(phi_ready, after(c, n, NPAIR, p + 1))
                            qh = p % 2
                            nc.scalar.activation(
                                ex[par][:, j, 2 * qh:2 * qh + 2, :].rearrange("p q g -> p (q g)"),
                                ps_phi[p % BANKS][:, 0:2 * G], ACT.Exp).then_inc(ex_ready, 1)
                    if on(c, l) and 1 <= j <= TG:
                        g = j - 1
                        act.wait_ge(xt_ps, after(c, l, TG, g + 1))
                        if not (early(c, l, 1) and g < 2):
                            act.wait_ge(main_done, after(c, l, TG, g - 1))
                        cols = P * (len(XGS[g]) - (g == TG - 1))
                        ins = nc.scalar.copy(xt[:, g % 2, 0:cols], ps_x[:, 0:cols])
                        if g == TG - 1:
                            rows = C0 - (CT - 1) * P
                            ins = nc.scalar.copy(xt[0:rows, g % 2, cols:cols + P], ps_x[0:rows, cols:cols + P])
                        ins.then_inc(xt_sb, 1)
                    if on(c, a) and j == 3:
                        act.wait_ge(logit_seq, after(c, a, 2, 2))
                        x = prob[1 - par][:].rearrange("p f g -> p (f g)")
                        nc.scalar.activation(x, x, ACT.Exp).then_inc(l0_exp, 1)
                    if on(c, l) and j == 6:
                        act.wait_ge(main_done, after(c, l, TG, TG))
                        act.wait_ge(z0_ps, after(c, l, 1, 0))
                        act.wait_ge(b_seq, after(c, l, KB, 0))
                        nc.scalar.copy(out0[:], ps_o[:, 0:J]).then_inc(out0_ready, 1)
                    if on(c, l) and j == 9:
                        act.wait_ge(z0_ps, after(c, l, 1, 1))
                        dst = z0_t[:].rearrange("p h (c q s) -> p h c q s", c=CH, q=Q)
                        dst = dst[:, :, bass.ds(chunk_of(c, l), 1), :, at(l)].rearrange("p h o q s -> p h (o q s)")
                        nc.scalar.copy(dst, ps_o[:, 256:256 + 2 * Q].rearrange("p (h q) -> p h q", h=2)).then_inc(z0_sb, 1)
                    if on(c, m) and j == GRP - 1:
                        sums(m, 0)
                    if on(c, k) and j == 2:
                        sums(k, 2)
                if on(c, m):
                    sums(m, 1)

            pipeline(act, tick)

        @block.tensor
        def _(pe):
            start_at_one(pe, xt_ps, main_done, z0_ps, phi_ready, z_ready, rrep_ready, s_ps)
            pe.wait_ge(consts_in, 16 * 15)
            pe.wait_ge(cleared, 5)

            def tick(c, h, t, par, part=None):
                n, m, k, l = t, t - 1, t - 2, t + 2

                def logits(p):
                    j, qh = divmod(p, 2)
                    kh, fg = divmod(j, FG)
                    if p == 0:
                        half = 16 * TERMS // 2
                        pe.wait_ge(t_in[par], after(c, n, half, 2 * half - half * par))
                    if qh == 0 and fg == 0:
                        pe.wait_ge(diag_ready, after(c, n, 2, kh + 1))
                    last = p - BANKS if p >= BANKS else max(x for x in range(NPAIR) if x % BANKS == p) - NPAIR
                    if last >= 0 or not early(c, n, 1):
                        pe.wait_ge(ex_ready, after(c, n, NPAIR, last + 1))
                    for i in range(2):
                        q = 2 * qh + i
                        mm = nc.tensor.matmul(ps_phi[p % BANKS][:, i * G:i * G + G], a_diag[:, kh, q, fg, :],
                                              t_rows[par][:, q * KH + kh, :], start=True, stop=True)
                    mm.then_inc(phi_ready, 1)

                def sum_f(j):
                    pe.wait_ge(ex_ready, after(c, n, NPAIR, 2 * j + 2))
                    if j == 0 and not early(c, n, 1):
                        pe.wait_ge(rz_ready, after(c, n, KR, 1 - KR))
                    for q in range(Q):
                        mm = nc.tensor.matmul(ps_z[K * q:K * q + K, 0:G], zsel[:, j // FG, :], ex[par][:, j, q, :],
                                              start=(j == 0), stop=(j == GRP - 1))
                    if j == GRP - 1:
                        mm.then_inc(z_ready, 1)

                def spread(r):
                    kh, qh = divmod(r, 2)
                    if r == 0:
                        pe.wait_ge(rz_ready, after(c, m, KR, KR))
                        if not early(c, m, 1):
                            pe.wait_ge(s_sb, after(c, m, NRND, -1))
                    pe.wait_ge(norm_done, after(c, m, 4, max(r - 1, 0)))
                    for i in range(2):
                        for part in range(PARTS):
                            mm = nc.tensor.matmul(ps_r[r % 2][:, i * G:i * G + G], rsel[:, (2 * qh + i) * KH + kh, :],
                                                  rz_split[:, part], start=(part == 0), stop=(part == PARTS - 1))
                    mm.then_inc(rrep_ready, 1)

                def sum_k(m, old, fg):
                    rnd = [fg in r for r in ROUNDS].index(True)
                    if fg == 0:
                        pe.wait_ge(norm_done, after(c, m, 4, 4))
                        pe.wait_ge(vst_ready, after(c, m, 1, 1))
                    if fg == ROUNDS[2][0]:
                        pe.wait_ge(s_sb, after(c, m, NRND, 0))
                    side = 256 * (fg - ROUNDS[rnd][0])
                    for kh in range(KH):
                        for q in range(Q):
                            mm = nc.tensor.matmul(
                                ps_sums[rnd][K * q:K * q + F8, side:side + G],
                                vst[old][:, (q * KH + kh) * FG + fg, :], ex[old][:, kh * FG + fg, q, :],
                                start=(kh == 0), stop=(kh == KH - 1))
                    if fg == ROUNDS[rnd][-1]:
                        mm.then_inc(s_ps, 1)

                def turn(g):
                    if g == 0:
                        pe.wait_ge(x_ready, after(c, l, 1, 1))
                    pe.wait_ge(xt_sb, after(c, l, TG, g))
                    x = prob[par][:].rearrange("p f g -> p (f g)")
                    for i, ct in enumerate(XGS[g]):
                        w = min(P, C0 - ct * P)
                        mm = nc.tensor.transpose(ps_x[0:w, i * P:i * P + P], x[:, ct * P:ct * P + w], ident[:])
                    mm.then_inc(xt_ps, 1)

                def layer1(g, tiles):
                    if 0 in tiles:
                        pe.wait_ge(xt_sb, after(c, l, TG, g + 1))
                    if g == 0:
                        pe.wait_ge(z0_sb, after(c, l, 1, 0))
                    for i in tiles:
                        ct = XGS[g][i]
                        w = min(P, C0 - ct * P)
                        mm = nc.tensor.matmul(ps_o[:, 0:J], xt[0:w, g % 2, i * P:i * P + P], cw0_sb[0:w, ct, :],
                                              start=(ct == 0), stop=(ct == CT - 1))
                    if i == len(XGS[g]) - 1:
                        mm.then_inc(main_done, 1)

                for j in range(GRP):
                    if on(c, n):
                        logits(2 * j)
                        logits(2 * j + 1)
                    if on(c, l) and j == 1:
                        turn(0)
                    if on(c, n) and j:
                        sum_f(j - 1)
                    if on(c, k) and j < len(ROUNDS[2]):
                        sum_k(k, par, ROUNDS[2][j])
                    if on(c, m):
                        if j == 1:
                            spread(0)
                            spread(1)
                    if on(c, l):
                        if 2 <= j <= TG:
                            turn(j - 1)
                        if 2 <= j <= TG:
                            layer1(j - 2, range(len(XGS[j - 2])))
                    if on(c, m) and j in (2, 3):
                        spread(j)
                    if on(c, l):
                        if j == TG + 1:
                            layer1(TG - 1, range(2))
                        if j == TG + 2:
                            layer1(TG - 1, range(2, len(XGS[TG - 1])))
                        if j == GRP - 1:
                            pe.wait_ge(out0_ready, after(c, l, 1, 1))
                            for h, j0, w in ZC:
                                mm = nc.tensor.matmul(ps_o[0:w, 256 + Q * h:256 + Q * h + Q], out0[:, j0:j0 + w],
                                                      onesq[:], start=True, stop=True)
                            mm.then_inc(z0_ps, 1)
                    if on(c, m) and j >= GRP - ROUNDS[2][0]:
                        sum_k(m, 1 - par, j - (GRP - ROUNDS[2][0]))
                if on(c, n):
                    sum_f(GRP - 1)

            pipeline(pe, tick)


def dense_layers(nc, dense_t, cw1, w1, b1, w2, b2, w3, scr_s, s_out, z0_t, z1_t, ident, reused, first_in, y):
    n1, n2 = H1 // P, H2 // P
    z_rows = [(0, z0_t, 0, P), (1, z0_t, 1, J - P), (2, z1_t, 0, P), (3, z1_t, 1, J - P + DD)]
    n_w = 9
    with ExitStack() as ctx:
        def sb(name, shape, dt=F32):
            return ctx.enter_context(nc.sbuf_tensor(name, shape, dt))

        def psum(name):
            return ctx.enter_context(nc.psum_tensor(name, [P, 512], F32))

        def sem(name):
            return ctx.enter_context(nc.semaphore(name))

        s_first, *cw1_pieces = first_operands(reused)
        n_first = len(cw1_pieces)
        cw1_pieces += [sb(f"cw1_piece{g // PIECE}", [R1, min(PIECE, GP - g), J]) for g in range(n_first * PIECE, GP, PIECE)]
        s_rows = [s_first, sb("s_rows1", [R1, P, GP])]
        w1_sb = sb("w1_sb", [P, 4, H1])
        w2_sb = sb("w2_sb", [P, n1, H2])
        w3_sb = sb("w3_sb", [P, n2])
        b1_sb = sb("b1_sb", [P, n1])
        b2_sb = sb("b2_sb", [P, n2])
        z1_b = sb("z1_b", [P, J])
        h1 = sb("h1", [P, n1, B])
        h2 = sb("h2", [P, n2, B])
        y_sb = sb("y_sb", [1, B])
        ps_z1 = psum("ps_z1")
        ps_t = psum("ps_t")
        ps_h = [psum(f"ps_h{i}") for i in range(4)]

        cw1_in = first_in[1:] + [sem(f"cw1_in{i}") for i in range(n_first, len(cw1_pieces))]
        srow_in = [first_in[0], sem("srow_in1")]
        weights_in = sem("weights_in")
        z1_ps = sem("z1_ps")
        z1_sb = sem("z1_sb")
        z1t_ps = sem("z1t_ps")
        z1t_sb = sem("z1t_sb")
        h_ps = sem("h_ps")
        h_sb = sem("h_sb")
        y_out = sem("y_out")

        block = ctx.enter_context(nc.Block())

        @block.sync
        def _(sp):
            for g in range(n_first * PIECE, GP, PIECE):
                w = min(PIECE, GP - g)
                sp.dma_start(cw1_pieces[g // PIECE][:], cw1[:, g:g + w]).then_inc(cw1_in[g // PIECE], 16)
            sp.dma_start(s_rows[1][:], scr_s[1]).then_inc(srow_in[1], 16)
            for i, r0, rows in ((0, 0, P), (1, P, J - P), (2, J, P), (3, J + P, J - P + DD)):
                sp.dma_start(w1_sb[0:rows, i], w1[r0:r0 + rows]).then_inc(weights_in, 16)
            for dst, src in ((w2_sb, w2), (w3_sb, w3), (b1_sb, b1), (b2_sb, b2)):
                sp.dma_start(dst[:], src).then_inc(weights_in, 16)
            sp.dma_start(z1_t[J - P:J - P + DD, 1], dense_t).then_inc(weights_in, 16)
            for c in range(2, CH):
                sp.wait_ge(z1_ps, c - 1)
                if c == CH - 1:
                    sp.wait_ge(s_out, CH * STEPS * 16 * Q + 1)
                sp.dma_start(s_rows[c % 2][:], scr_s[c]).then_inc(srow_in[c % 2], 16)
            sp.wait_ge(h_sb, n1 + n2 + 1)
            sp.dma_start(y, y_sb[:]).then_inc(y_out, 16)
            sp.wait_ge(y_out, 16)

        @block.tensor
        def _(pe):
            pe.sem_inc(z1t_ps, 1)

            def turn(c):
                pe.wait_ge(z1_sb, c + 2)
                pe.wait_ge(z1t_sb, c + 1)
                for h, j0, w in ZC:
                    mm = nc.tensor.transpose(ps_t[0:w, h * P:h * P + P], z1_b[:, j0:j0 + w], ident[:])
                mm.then_inc(z1t_ps, 1)

            with pe.Fori(0, CH // 2) as pair:
                for i in range(2):
                    c = pair * 2 + i
                    pe.wait_ge(srow_in[i], pair * 16 + 16)
                    pe.wait_ge(z1_sb, c + 1)
                    for g in range(GP):
                        if g % PIECE == 0:
                            pe.wait_ge(cw1_in[g // PIECE], 16)
                        mm = nc.tensor.matmul(ps_z1[:, 0:J], s_rows[i][:, :, g], cw1_pieces[g // PIECE][:, g % PIECE, :],
                                              start=(g == 0), stop=(g == GP - 1))
                    mm.then_inc(z1_ps, 1)
                    turn(c)
            pe.wait_ge(weights_in, 16 * n_w)
            pe.wait_ge(z1t_sb, CH + 1)
            for m in range(n1):
                for i, z, h, rows in z_rows:
                    mm = nc.tensor.matmul(ps_h[m % 4][:], w1_sb[0:rows, i, m * P:m * P + P], z[0:rows, h, :],
                                          start=(i == 0), stop=(i == len(z_rows) - 1))
                mm.then_inc(h_ps, 1)
            pe.wait_ge(h_sb, n1)
            for m in range(n2):
                for i in range(n1):
                    mm = nc.tensor.matmul(ps_h[m][:], w2_sb[:, i, m * P:m * P + P], h1[:, i, :],
                                          start=(i == 0), stop=(i == n1 - 1))
                mm.then_inc(h_ps, 1)
            pe.wait_ge(h_sb, n1 + n2)
            for m in range(n2):
                mm = nc.tensor.matmul(ps_h[2][0:1, :], w3_sb[:, m:m + 1], h2[:, m, :], start=(m == 0), stop=(m == n2 - 1))
            mm.then_inc(h_ps, 1)

        @block.scalar
        def _(act):
            act.sem_inc(z1_sb, 1)
            act.sem_inc(z1t_sb, 1)
            with act.Fori(0, CH) as c:
                act.wait_ge(z1_ps, c + 1)
                act.wait_ge(z1t_ps, c + 1)
                nc.scalar.copy(z1_b[:], ps_z1[:, 0:J]).then_inc(z1_sb, 1)
                act.wait_ge(z1t_ps, c + 2)
                for h, j0, w in ZC:
                    ins = nc.scalar.copy(z1_t[0:w, h, bass.ds(c * P, P)], ps_t[0:w, h * P:h * P + P])
                ins.then_inc(z1t_sb, 1)
            act.wait_ge(weights_in, 16 * n_w)
            for m in range(n1):
                act.wait_ge(h_ps, m + 1)
                nc.scalar.activation(h1[:, m, :], ps_h[m % 4][:], ACT.Relu, bias=b1_sb[:, m:m + 1]).then_inc(h_sb, 1)
            for m in range(n2):
                act.wait_ge(h_ps, n1 + m + 1)
                nc.scalar.activation(h2[:, m, :], ps_h[m][:], ACT.Relu, bias=b2_sb[:, m:m + 1]).then_inc(h_sb, 1)
            act.wait_ge(h_ps, n1 + n2 + 1)
            nc.scalar.copy(y_sb[:], ps_h[2][0:1, :]).then_inc(h_sb, 1)


def kernel(**inputs):
    import ml_dtypes
    import numpy as np
    import concourse.bacc as bacc
    from concourse.bass_utils import run_bass_kernel_spmd

    x = {k: np.asarray(v) for k, v in inputs.items()}
    p = np.arange(P)
    zsel = np.zeros((P, KH, K), np.float32)
    rsel = np.zeros((P, U, P), np.float32)
    for kh in range(KH):
        zsel[p, kh, kh * KL + p // F8] = 1
    for u in range(U):
        rsel[u * KL + p // F8, u, p] = 1
    diag = (p[:, None, None] % KL == np.arange(KL)[None, :, None]) * np.ones((1, 1, F8))
    f8sel = (p[:, None] % F8 == np.arange(F8)[None]) * 1.0
    onesq = (p[:, None] // K == np.arange(Q)[None]) * 1.0

    def rows(name):
        return x["L0_rec_" + name][0].T

    cw0 = np.pad(x["L0_rec_cw0"][0], ((0, CT * P - C0), (0, 0))).reshape(CT, P, J).transpose(1, 0, 2)
    cw1 = np.pad(x["L0_rec_cw1"][0].reshape(F8, FG, G, J), ((0, 0), (0, 0), (0, GT * GP - G), (0, 0)))
    cw1 = cw1.reshape(F8, FG, GT, GP, J).transpose(2, 1, 0, 3, 4).reshape(R1, GP, J)
    arrays = {
        "dense_t": x["dense_ctx"].T, "ids": np.concatenate([x["ids"], x["ids"][:P]]).reshape(CH + 1, P, F),
        "w_k": np.stack([rows("wk0"), rows("wq0"), rows("wv0"), rows("wk1"), rows("wv1")], 1), "wq1_t": rows("wq1"),
        "cw0": cw0, "cw1": cw1, "w1": x["W_top1"], "b1": x["b_top1"].reshape(-1, P).T,
        "w2": x["W_top2"].reshape(-1, P, H2).transpose(1, 0, 2), "b2": x["b_top2"].reshape(-1, P).T,
        "w3": x["W_top3"].reshape(-1, P).T, "ident": np.eye(P, dtype=np.float32), "zsel": zsel, "rsel": rsel.astype(ml_dtypes.bfloat16),
        "diag": diag.astype(ml_dtypes.bfloat16), "f8sel": f8sel.astype(np.float32), "onesq": onesq.astype(np.float32),
    }
    arrays.update({f"tbl_{f}": x[f"tbl_{f}"] for f in range(F)})
    arrays = {k: np.ascontiguousarray(v) for k, v in arrays.items()}
    nc = bacc.Bacc("TRN2", target_bir_lowering=False, num_devices=1)
    d = {k: nc.dram_tensor("in_" + k, v.shape, mybir.dt.from_np(v.dtype), kind="ExternalInput").ap() for k, v in arrays.items()}
    y = nc.dram_tensor("y", (1, B), F32, kind="ExternalOutput").ap()
    dlrm_cin_tower(nc, d["dense_t"], d["ids"], [d[f"tbl_{f}"] for f in range(F)], d["w_k"], d["wq1_t"], d["cw0"],
                   d["cw1"], d["w1"], d["b1"], d["w2"], d["b2"], d["w3"], d["ident"], d["zsel"], d["rsel"],
                   d["diag"], d["f8sel"], d["onesq"], y)
    r = run_bass_kernel_spmd(nc, [{"in_" + k: v for k, v in arrays.items()}], core_ids=[0])
    return r.results[0]["y"].reshape(B, 1)
```
